# Optimizing a Trainium2 kernel written in Bass

```python
import numpy as np
import jax
import jax.numpy as jnp

def _softmax(x, axis=-1):
    return jax.nn.softmax(x, axis=axis)

def _gelu(x):
    return jax.nn.gelu(x, approximate=True)

def _silu(x):
    return jax.nn.silu(x)

def _sigmoid(x):
    return jax.nn.sigmoid(x)

def _layernorm(x, axis=-1, eps=1e-05):
    m = jnp.mean(x, axis=axis, keepdims=True)
    v = jnp.var(x, axis=axis, keepdims=True)
    return (x - m) / jnp.sqrt(v + eps)

def _scatter_add(tgt, idx, src, axis=0):
    return tgt.at[idx].add(src)

def _segment_sum(src, seg, n):
    return jax.ops.segment_sum(src, seg, n)
kernel_name = 'mk_xattn_ffn_d1_seqx_r4_268c5f'

def setup_inputs(seed: int=0):
    np.random.seed(seed)
    _w = jnp.asarray

    def _rec_inputs():
        import jax
        import jax.numpy as jnp
        _rk = jax.random.key(seed)
        x = -0.0002928 + 1 * jax.random.normal(jax.random.fold_in(_rk, 1), (2, 1024, 256), jnp.float32)
        _lenS = 1024 - jax.random.randint(jax.random.fold_in(_rk, 7), (2,), 0, max(1, 1024 // 4) + 1, jnp.int32)
        _lenS2 = 77 - jax.random.randint(jax.random.fold_in(_rk, 8), (2,), 0, max(1, 77 // 4) + 1, jnp.int32)
        _ctx_1024P = jax.random.normal(jax.random.fold_in(_rk, 11), (2, 16, 256), jnp.float32)
        _ctx_1024c = jax.random.dirichlet(jax.random.fold_in(_rk, 511), 0.3 * jnp.ones((16,), jnp.float32), (2, 77))
        _ctx_1024t = jnp.einsum('bsk,bkd->bsd', _ctx_1024c, _ctx_1024P)
        _ctx_1024t = _ctx_1024t * jax.lax.rsqrt(jnp.mean(jnp.square(_ctx_1024t)) + 1e-12) * 0.953939
        ctx_1024 = -1.39393e-06 + 0.999914 * (_ctx_1024t + 0.3 * jax.random.normal(jax.random.fold_in(_rk, 611), (2, 77, 256), jnp.float32))
        _validS = jnp.arange(1024)[None, :] < _lenS[:, None]
        _validS2 = jnp.arange(77)[None, :] < _lenS2[:, None]
        _causal = jnp.tril(jnp.ones((1024, 1024), dtype=bool))
        mask_BxSxS2_bk1 = jnp.broadcast_to(_validS2[:, None, :], (2, 1024, 77))
        return (x, ctx_1024, mask_BxSxS2_bk1)
    x, ctx_1024, mask_BxSxS2_bk1 = _rec_inputs()

    def _L0_xattn_setup():
        import jax, jax.numpy as jnp
        import numpy as np
        DIM = 256
        HEADS = 16
        DIM_HEAD = 64
        INNER = HEADS * DIM_HEAD
        B, N = (2, 512)
        key = jax.random.key(seed)
        ks = jax.random.split(key, 8)
        q = jax.random.normal(ks[0], (B, N, DIM), dtype=jnp.float32)
        k = jax.random.normal(ks[1], (B, N, DIM), dtype=jnp.float32)
        v = jax.random.normal(ks[2], (B, N, DIM), dtype=jnp.float32)
        causal = jnp.triu(jnp.ones((N, N), dtype=jnp.bool_), k=1)
        mask = jnp.broadcast_to(causal, (B, N, N))
        s = 0.02
        Wq = jax.random.normal(ks[3], (DIM, INNER), dtype=jnp.float32) * s
        Wk = jax.random.normal(ks[4], (DIM, INNER), dtype=jnp.float32) * s
        Wv = jax.random.normal(ks[5], (DIM, INNER), dtype=jnp.float32) * s
        Wo = jax.random.normal(ks[6], (INNER, DIM), dtype=jnp.float32) * s
        bo = jnp.zeros((DIM,), dtype=jnp.float32)
        return {'q': q, 'k': k, 'v': v, 'mask': mask, 'Wq': Wq, 'Wk': Wk, 'Wv': Wv, 'Wo': Wo, 'bo': bo}
    _L0_xattn_all = _L0_xattn_setup()
    _L0_xattn_in = {k: v for k, v in _L0_xattn_all.items() if k in ('Wq', 'Wk', 'Wv', 'Wo', 'bo')}
    del _L0_xattn_all

    def _L0_ffn_setup():
        import jax, jax.numpy as jnp
        import numpy as np
        TOP_K = 2
        ROUTE_SCALE = 1.0
        EPS = 1e-20
        key = jax.random.key(seed)
        ks = jax.random.split(key, 8)
        dim, hid, E, X = (256, 704, 8, 1)
        std = 0.02
        x = jax.random.normal(ks[0], (2, 512, dim), dtype=jnp.float32)
        w1 = jax.random.normal(ks[1], (E, hid, dim), dtype=jnp.float32) * std
        w2 = jax.random.normal(ks[2], (E, dim, hid), dtype=jnp.float32) * std
        w3 = jax.random.normal(ks[3], (E, hid, dim), dtype=jnp.float32) * std
        new_w1 = jax.random.normal(ks[4], (X, hid, dim), dtype=jnp.float32) * std
        new_w2 = jnp.zeros((X, dim, hid), dtype=jnp.float32)
        new_w3 = jax.random.normal(ks[5], (X, hid, dim), dtype=jnp.float32) * std
        gate_weight = jax.random.normal(ks[6], (E, dim), dtype=jnp.float32) * std
        new_gate_weight = jax.random.normal(ks[7], (X, dim), dtype=jnp.float32) * std
        gate_bias = jnp.zeros((X,), dtype=jnp.float32)
        return dict(x=x, w1=w1, w2=w2, w3=w3, new_w1=new_w1, new_w2=new_w2, new_w3=new_w3, gate_weight=gate_weight, new_gate_weight=new_gate_weight, gate_bias=gate_bias)
    _L0_ffn_all = _L0_ffn_setup()
    _L0_ffn_in = {k: v for k, v in _L0_ffn_all.items() if k in ('w1', 'w2', 'w3', 'new_w1', 'new_w2', 'new_w3', 'gate_weight', 'new_gate_weight', 'gate_bias')}
    del _L0_ffn_all
    return {'x': x, 'ctx_1024': ctx_1024, 'mask_BxSxS2_bk1': mask_BxSxS2_bk1, 'L0_xattn_Wq': _L0_xattn_in['Wq'], 'L0_xattn_Wk': _L0_xattn_in['Wk'], 'L0_xattn_Wv': _L0_xattn_in['Wv'], 'L0_xattn_Wo': _L0_xattn_in['Wo'], 'L0_xattn_bo': _L0_xattn_in['bo'], 'L0_ffn_w1': _L0_ffn_in['w1'], 'L0_ffn_w2': _L0_ffn_in['w2'], 'L0_ffn_w3': _L0_ffn_in['w3'], 'L0_ffn_new_w1': _L0_ffn_in['new_w1'], 'L0_ffn_new_w2': _L0_ffn_in['new_w2'], 'L0_ffn_new_w3': _L0_ffn_in['new_w3'], 'L0_ffn_gate_weight': _L0_ffn_in['gate_weight'], 'L0_ffn_new_gate_weight': _L0_ffn_in['new_gate_weight'], 'L0_ffn_gate_bias': _L0_ffn_in['gate_bias']}

def reference(x, ctx_1024, mask_BxSxS2_bk1, L0_xattn_Wq, L0_xattn_Wk, L0_xattn_Wv, L0_xattn_Wo, L0_xattn_bo, L0_ffn_w1, L0_ffn_w2, L0_ffn_w3, L0_ffn_new_w1, L0_ffn_new_w2, L0_ffn_new_w3, L0_ffn_gate_weight, L0_ffn_new_gate_weight, L0_ffn_gate_bias):
    import jax
    import jax.numpy as jnp

    def _L0_xattn_ref(q, k, v, mask, Wq, Wk, Wv, Wo, bo):
        import jax, jax.numpy as jnp
        import numpy as np
        DIM = 256
        HEADS = 16
        DIM_HEAD = 64
        INNER = HEADS * DIM_HEAD
        B, N = (2, 512)
        h, d = (HEADS, DIM_HEAD)
        scale = d ** (-0.5)
        b, n, _ = q.shape

        def heads_split(x):
            return x.reshape(b, -1, h, d).transpose(0, 2, 1, 3)
        qh = heads_split(q @ Wq)
        kh = heads_split(k @ Wk)
        vh = heads_split(v @ Wv)
        dots = jnp.einsum('bhid,bhjd->bhij', qh, kh) * scale
        mask_value = -jnp.finfo(dots.dtype).max
        dots = jnp.where(mask[:, None, :, :], mask_value, dots)
        attn = jax.nn.softmax(dots, axis=-1)
        out = jnp.einsum('bhij,bhjd->bhid', attn, vh)
        out = out.transpose(0, 2, 1, 3).reshape(b, n, h * d)
        out = out @ Wo + bo
        return out

    def _L0_ffn_ref(x, w1, w2, w3, new_w1, new_w2, new_w3, gate_weight, new_gate_weight, gate_bias):
        import jax, jax.numpy as jnp
        import numpy as np
        TOP_K = 2
        ROUTE_SCALE = 1.0
        EPS = 1e-20
        bs, slen, dim = x.shape
        x_flat = x.reshape(-1, dim)
        ew1 = jnp.concatenate([w1, new_w1], axis=0)
        ew2 = jnp.concatenate([w2, new_w2], axis=0)
        ew3 = jnp.concatenate([w3, new_w3], axis=0)
        gate = jnp.concatenate([gate_weight, new_gate_weight], axis=0)
        e_orig = w1.shape[0]
        e_tot = gate.shape[0]
        bias = jnp.concatenate([jnp.zeros((e_orig,), x.dtype), gate_bias])
        scores = jax.nn.sigmoid((x_flat @ gate.T + bias).astype(jnp.float32))
        top_scores, selected = jax.lax.top_k(scores, TOP_K)
        top_scores = top_scores / (jnp.sum(top_scores, axis=-1, keepdims=True) + EPS)
        top_scores = top_scores * ROUTE_SCALE
        onehot = jax.nn.one_hot(selected, e_tot, dtype=jnp.float32)
        cw = jnp.einsum('tk,tke->te', top_scores, onehot)
        out = jnp.zeros_like(x_flat)
        for e in range(e_tot):
            h = jax.nn.silu(x_flat @ ew1[e].T) * (x_flat @ ew3[e].T)
            out = out + cw[:, e:e + 1] * (h @ ew2[e].T)
        return out.reshape(bs, slen, dim)
    x = x + _L0_xattn_ref(_layernorm(x, axis=-1), ctx_1024, ctx_1024, mask_BxSxS2_bk1, L0_xattn_Wq, L0_xattn_Wk, L0_xattn_Wv, L0_xattn_Wo, L0_xattn_bo)
    x = x + _L0_ffn_ref(_layernorm(x, axis=-1), L0_ffn_w1, L0_ffn_w2, L0_ffn_w3, L0_ffn_new_w1, L0_ffn_new_w2, L0_ffn_new_w3, L0_ffn_gate_weight, L0_ffn_new_gate_weight, L0_ffn_gate_bias)
    return x

_drawn_inputs = setup_inputs


def setup_inputs(seed=0):
    import zlib

    import numpy as np

    out = dict(_drawn_inputs(seed))
    spreads = {'L0_xattn_bo': (0.0, 0.1), 'L0_ffn_new_w2': (0.0, 0.273)}
    factors = {'L0_xattn_Wq': 6.908,
     'L0_xattn_Wk': 6.908,
     'L0_ffn_w1': 2.95,
     'L0_ffn_w2': 2.789,
     'L0_ffn_w3': 2.767}
    for name, (base, spread) in spreads.items():
        noise = np.random.default_rng([zlib.crc32(name.encode()), seed]).standard_normal(out[name].shape)
        drawn = base * np.exp(spread * noise) if base else spread * noise
        out[name] = jnp.asarray(drawn.astype(out[name].dtype))
    for name, factor in factors.items():
        out[name] = (out[name] * factor).astype(out[name].dtype)
    return out
```

```python
from contextlib import ExitStack

import numpy as np

import concourse.bass as bass
from concourse import mybir

F32, F16, BF16 = mybir.dt.float32, mybir.dt.float16, mybir.dt.bfloat16
I32, U32, U8 = mybir.dt.int32, mybir.dt.uint32, mybir.dt.uint8
ALU = mybir.AluOpType
ACT = mybir.ActivationFunctionType
AX = mybir.AxisListType

P = 128
B, N, D = 2, 1024, 256
T = B * N
J = 77
HEADS, DH = 16, 64
INNER = HEADS * DH
HJ = HEADS * J
HJP = 1280
NCH = HJP // P
KD = D // P
E9 = 9
HID = 704
HC = 6
NT = T // P
TPB = NT // B
NF = (2 * T - E9) // P + E9
TR = T + P
W13C = KD * 2 * HID
WC = W13C + HC * D
EARLY = 6
QC = WC // 4
SC_H = [6, 6, 4]
LN_EPS = 1e-5
SP_P, SP_B, SP_W = 1024.0, 64.0, 64.0
MASKED = -3.0e38
Z_ONE = 16.635532
C_ID, C_TRI, C_IOTA, C_REV, C_LT, C_TOK, C_P = 0, 128, 256, 384, 393, 474, 490
C_ALL = 491


def at_least(eng, sem, n):
    if isinstance(n, int) and n <= 0:
        return
    eng.wait_ge(sem, n)


def pipeline(eng, step, first, last, lo, hi):
    for s in range(first, lo):
        step(s, s)
    with eng.Fori(0, (hi - lo) // 2) as j:
        for u in range(2):
            step(j * 2 + (lo + u), lo + u)
    for s in range(hi, last):
        step(s, s)


def build(nc, x, ctxT, mask, wq, wk, wv, wo, bo, wt, gate, gbias, consts, out):
    with ExitStack() as ctx:
        def sb(name, shape, dt):
            return ctx.enter_context(nc.sbuf_tensor(name, shape, dt))

        def sem(name):
            return ctx.enter_context(nc.semaphore(name))

        def sems(name, n):
            return [sem(f"{name}{k}") for k in range(n)]

        acc = nc.dram_tensor("acc_rows", [TR, D], F32, kind="Internal").ap()
        xn2_rows = nc.dram_tensor("xn2_rows", [TR, D], F32, kind="Internal").ap()
        b_rows = nc.dram_tensor("b_rows", [2, B, HJ, D], F16, kind="Internal").ap()

        w_all = sb("w_all", [P, E9 * 2 * WC], F16)
        con = sb("con", [P, C_ALL], F32)
        idb = sb("idb", [P, P], BF16)
        trib = sb("trib", [P, P], BF16)
        onesb = sb("onesb", [P, P], BF16)
        iota16 = sb("iota16", [P, P], F16)
        bo_b = sb("bo_b", [P, D], F32)
        gb_b = sb("gb_b", [P, E9], F32)
        gate_sb = sb("gate_sb", [P, KD, E9], F32)
        mv_all = sb("mv_all", [P, NT, 2], F32)
        rstd_all = sb("rstd_all", [P, NT], F32)
        mhalf = sb("mhalf", [P, NT], F32)
        lg = sb("lg", [P, NT, E9], F32)
        idx_all = sb("idx_all", [P, NF], U32)
        cw_all = sb("cw_all", [P, NF], F32)
        eid = sb("eid", [P, NF], I32)
        stage = sb("stage", [P, 4, QC], F32)
        WORK = 28000
        work = sb("work", [P, WORK], mybir.dt.uint8)
        ps = ctx.enter_context(nc.psum_tensor("ps", [P, 8, 512], F32))

        def view(base, off, shape, dt):
            n = int(np.prod(shape)) * mybir.dt.size(dt)
            v = base[:, off:off + n].bitcast(dt)
            names = "abcd"[:len(shape)]
            if len(shape) > 1:
                v = v.rearrange(f"p ({' '.join(names)}) -> p {' '.join(names)}", **dict(zip(names[1:], shape[1:])))
            return v, off + n

        LATE = EARLY * 2 * WC
        late = w_all[:, LATE:]

        def lview(off, shape, dt):
            n = int(np.prod(shape)) * mybir.dt.size(dt)
            v = late[:, off // 2:(off + n) // 2].bitcast(dt)
            names = "abcd"[:len(shape)]
            if len(shape) > 1:
                v = v.rearrange(f"p ({' '.join(names)}) -> p {' '.join(names)}", **dict(zip(names[1:], shape[1:])))
            return v, off + n

        o = 0
        a_hi, o = lview(o, [KD, B, HJ], F16)
        a_lo, o = lview(o, [KD, B, HJ], F16)
        b_hi, o = lview(o, [B, NCH, D], F16)
        b_lo, o = lview(o, [B, NCH, D], F16)
        maskb, o = lview(o, [NT, J], BF16)
        mask32, o = lview(o, [NT * J // 4], U32)
        mask8 = mask32.bitcast(U8).rearrange("p (i j) -> p i j", j=J)
        ebuf0, o = lview(o, [HJP], F32)
        x_h, o = lview(o, [2, KD, P], F16)
        x_l, o = lview(o, [2, KD, P], F16)
        assert o <= 3 * 2 * WC * 2, o
        o = 0
        ebuf1, o = view(work, o, [HJP], F32)
        pt_h, o = view(work, o, [NCH, P], F16)
        pt_l, o = view(work, o, [NCH, P], F16)
        xbuf, o = view(work, o, [2, D], F32)
        xrb, o = view(work, o, [2, D], F32)
        xnb, o = view(work, o, [2, D], F32)
        x1b, o = view(work, o, [2, D], F32)
        xn2b, o = view(work, o, [2, D], F32)
        xn2t, o = view(work, o, [2, KD, P], F32)
        mx, o = view(work, o, [2, HEADS], F32)
        rs, o = view(work, o, [2, HEADS], F32)
        rr, o = view(work, o, [2, HEADS], F32)
        st6, o = view(work, o, [2, 6], F32)
        mv2, o = view(work, o, [2, 2], F32)
        ve2, o = view(work, o, [2, 1], F32)
        rstd2, o = view(work, o, [2, 1], F32)
        assert o <= WORK, o
        ebuf = [ebuf0, ebuf1]
        o = 0
        xg, o = view(work, o, [2, D], F32)
        fx_h, o = view(work, o, [2, KD, P], F16)
        fx_l, o = view(work, o, [2, KD, P], F16)
        sg, o = view(work, o, [2, HID], F32)
        hb, o = view(work, o, [2, HC * P], F32)
        ht_h, o = view(work, o, [HC, P], F16)
        ht_l, o = view(work, o, [HC, P], F16)
        yb, o = view(work, o, [2, D], F32)
        idg, o = view(work, o, [2, 1], U32)
        ids, o = view(work, o, [2, 1], U32)
        assert o <= WORK, o
        pro = w_all[:, 2 * WC:LATE]

        def pview(off, shape, dt):
            n = int(np.prod(shape)) * mybir.dt.size(dt)
            v = pro[:, off // 2:(off + n) // 2].bitcast(dt)
            names = "abcd"[:len(shape)]
            if len(shape) > 1:
                v = v.rearrange(f"p ({' '.join(names)}) -> p {' '.join(names)}", **dict(zip(names[1:], shape[1:])))
            return v, off + n

        o = 0
        wq_sb, o = pview(o, [INNER // P, D], F32)
        wk_sb, o = pview(o, [KD, INNER], F32)
        wv_sb, o = pview(o, [KD, INNER], F32)
        wo_sb, o = pview(o, [INNER // P, D], F32)
        ctx_sb, o = pview(o, [KD, B * J], F32)
        kt_sb, o = pview(o, [INNER // P, B * J], F32)
        vt_sb, o = pview(o, [INNER // P, B * J], F32)
        bs_h, o = pview(o, [B, HEADS, D], F16)
        bs_l, o = pview(o, [B, HEADS, D], F16)
        assert o <= 5 * 2 * WC * 2, o
        x_all = w_all[:, 0:NT * D * 2].bitcast(F32).rearrange("p (i d) -> p i d", d=D)
        R = {}
        o = 0
        for name, shape, dt in [
            ("m", [2, NT], F32), ("sgm", [2, NT], F32), ("c", [2, NT], F32), ("wsum", [NT], F32), ("wrec", [NT], F32),
            ("cwv", [2, NT], F32), ("eq", [NT, E9], F32), ("oh1", [NT, E9], F32), ("oh2", [NT, E9], F32),
            ("lg2", [NT, E9], F32), ("s16", [NT + 1, E9], BF16), ("cnt", [E9 + 1], F32), ("cnti", [E9 + 1], I32),
            ("ntl", [E9 + 1], F32), ("cmul", [E9, E9], F32), ("cin", [E9 + 1], F32), ("cex", [E9 + 1], F32),
            ("slot", [NT, E9], F32), ("sel", [NT, E9], F32), ("sl", [2, NT], F32), ("sli", [2, NT], I32),
            ("pi", [2, NT], I32), ("ti", [2, NT], I32), ("pf", [2 * NT], F32), ("tf", [2 * NT], F32),
            ("val", [3, 2 * NT], F32), ("ueq", [2 * NT, NF], F16), ("u", [2 * NT, 3, NF], F16),
            ("pad", [NF], F32), ("idf", [NF], F32), ("idf2", [NF], F32), ("cws", [NF], F32), ("ecmp", [NF, E9], F32),
            ("ef", [NF], F32), ("vhot", [2 * NT, P], F16),
        ]:
            if name == "val":
                o = (o + 3) // 4 * 4
            R[name], o = view(work, o, shape, dt)
            o = (o + 3) // 4 * 4
        assert o <= WORK, o
        vhot = R["vhot"]

        con_in, bc_in, ctx_in, wk_in, wq_in, wv_in, wo_in, mask_in = (sem(n) for n in (
            "con_in", "bc_in", "ctx_in", "wk_in", "wq_in", "wv_in", "wo_in", "mask_in"))
        xall_in = sem("xall_in")
        setup = sem("setup")
        cpy = sem("cpy")
        mask_ok = sem("mask_ok")
        stats1, stat1_ok, rstd1 = sem("stats1"), sem("stat1_ok"), sem("rstd1")
        kv_mm, kv_ev = sem("kv_mm"), sem("kv_ev")
        a_mm, a_hi_ok, a_lo_ok = sem("a_mm"), sem("a_hi_ok"), sem("a_lo_ok")
        b_mm, b_hi_ok, b_lo_ok = sem("b_mm"), sem("b_hi_ok"), sem("b_lo_ok")
        b_out, b_in = sem("b_out"), sem("b_in")
        w_in = sems("w_in", 4)
        w_sc_ok, w_hi_ok, w_lo_ok = sem("w_sc_ok"), sem("w_hi_ok"), sem("w_lo_ok")
        x_in, xr_in = sems("x_in", 2), sems("xr_in", 2)
        x1_out, xn2_out = sems("x1_out", 2), sems("xn2_out", 2)
        xn_ok, xt_mm, xh_ok, xl_ok, sc_mm = (sem(n) for n in ("xn_ok", "xt_mm", "xh_ok", "xl_ok", "sc_mm"))
        max_ok, sub_ok, exp_ok, sum_ok, rec_ok, norm_ok = (sem(n) for n in (
            "max_ok", "sub_ok", "exp_ok", "sum_ok", "rec_ok", "norm_ok"))
        pt_mm, ph_ok, pl_ok, out_mm, xb_ok, x1_ok = (sem(n) for n in ("pt_mm", "ph_ok", "pl_ok", "out_mm", "xb_ok", "x1_ok"))
        st_ok, mv_ok, ve_ok, rstd_ok, xn2_ok = (sem(n) for n in ("st_ok", "mv_ok", "ve_ok", "rstd_ok", "xn2_ok"))
        xn2t_mm, xn2t_ok, gate_mm, lg_ok = (sem(n) for n in ("xn2t_mm", "xn2t_ok", "gate_mm", "lg_ok"))
        rt = sem("rt")
        s16_ok, rank_mm, sig_ok, m_ok, v_ok, u_ok, map_mm, route_ok = (sem(n) for n in (
            "s16_ok", "rank_mm", "sig_ok", "m_ok", "v_ok", "u_ok", "map_mm", "route_ok"))
        zero_ok, zero_out = sem("zero_ok"), sem("zero_out")
        g_in, s_out = sems("g_in", 2), sems("s_out", 2)
        idg_ok, ids_ok, hpad_ok = sem("idg_ok"), sem("ids_ok"), sem("hpad_ok")
        fxt_mm, fxh_ok, fxl_ok, w13_mm, silu_ok, h_ok = (sem(n) for n in (
            "fxt_mm", "fxh_ok", "fxl_ok", "w13_mm", "silu_ok", "h_ok"))
        fht_mm, fhh_ok, fhl_ok, w2_mm, y_ok = (sem(n) for n in ("fht_mm", "fhh_ok", "fhl_ok", "w2_mm", "y_ok"))
        dma_go, done = sem("dma_go"), sem("done")

        xv = x.rearrange("(i p) d -> i p d", p=P)
        LAG_OUT, LAG_X1, LAG_XN2, LAG_G = 2, 3, 4, 5
        A_FIRST, A_LAST = -2, NT + LAG_G + 1
        A_LO, A_HI = 6, 14

        def on(s, lag):
            return 0 <= s - lag < NT

        def pipe_a(eng, step):
            pipeline(eng, step, A_FIRST, A_LAST, A_LO, A_HI)

        def cap(n):
            return min(n, NT) if isinstance(n, int) else n

        F_FIRST, F_LAST, F_LO, F_HI = -2, NF + 4, 6, NF - 2

        def onf(s, lag):
            return 0 <= s - lag < NF

        def pipe_f(eng, step):
            pipeline(eng, step, F_FIRST, F_LAST, F_LO, F_HI)

        def w_chunk(q, plane):
            e, part = q // 4, q % 4
            base = e * 2 * WC + plane * WC + part * QC
            return w_all[:, base:base + QC]

        block = ctx.enter_context(nc.Block())

        @block.sync
        def _(sp):
            sp.dma_start(con[:], consts).then_inc(con_in, 16)
            sp.dma_start(ctx_sb, ctxT.rearrange("(k p) j -> p k j", p=P)).then_inc(ctx_in, 16)
            sp.dma_start(wk_sb, wk.rearrange("(k p) n -> p k n", p=P)).then_inc(wk_in, 16)
            sp.dma_start(wq_sb, wq.rearrange("(m p) n -> p m n", p=P)).then_inc(wq_in, 16)
            sp.dma_start(x_all, x.rearrange("(i p) d -> p i d", p=P)).then_inc(xall_in, 16)
            sp.dma_start(mask32, mask).then_inc(mask_in, 16)
            sp.dma_start(wv_sb, wv.rearrange("(k p) n -> p k n", p=P)).then_inc(wv_in, 16)
            sp.dma_start(wo_sb, wo.rearrange("(m p) n -> p m n", p=P)).then_inc(wo_in, 16)
            sp.dma_start(bo_b[:], bo.partition_broadcast(P)).then_inc(bc_in, 16)
            sp.dma_start(gb_b[:], gbias.partition_broadcast(P)).then_inc(bc_in, 16)
            sp.dma_start(gate_sb[:], gate.rearrange("(k p) e -> p k e", p=P)).then_inc(bc_in, 16)
            sp.wait_ge(zero_ok, 1)
            sp.dma_start(acc[T:TR, :], xnb[:, 0]).then_inc(zero_out, 16)
            sp.dma_start(xn2_rows[T:TR, :], xnb[:, 0]).then_inc(zero_out, 16)

            def load_w(q):
                at_least(sp, w_lo_ok, q - 3)
                sp.dma_start(stage[:, q % 4, :], wt[q // 4, :, (q % 4) * QC:(q % 4 + 1) * QC]).then_inc(w_in[q % 4], 16)

            def load_x(i, par):
                at_least(sp, xn_ok, i - 1)
                sp.dma_start(xbuf[:, par], xv[i]if isinstance(i, int) else x[bass.ds(i * P, P), :]).then_inc(x_in[par], 16)

            def load_xr(i, par):
                at_least(sp, x1_ok, i - 1)
                sp.dma_start(xrb[:, par], xv[i]if isinstance(i, int) else x[bass.ds(i * P, P), :]).then_inc(xr_in[par], 16)

            def store(i, par):
                rows = slice(i * P, (i + 1) * P) if isinstance(i, int) else bass.ds(i * P, P)
                at_least(sp, x1_ok, i + 1)
                sp.dma_start(acc[rows, :], x1b[:, par]).then_inc(x1_out[par], 16)
                at_least(sp, xn2_ok, i + 1)
                sp.dma_start(xn2_rows[rows, :], xn2b[:, par]).then_inc(xn2_out[par], 16)

            def b_store():
                sp.wait_ge(b_lo_ok, HEADS)
                sp.wait_ge(b_hi_ok, HEADS)
                for pl, src in enumerate((bs_h, bs_l)):
                    for b in range(B):
                        sp.dma_start(b_rows[pl, b].rearrange("(h j) d -> j h d", j=J), src[0:J, b]).then_inc(b_out, 16)
                sp.wait_ge(b_out, 16 * 4)
                for pl, dst in enumerate((b_hi, b_lo)):
                    for b in range(B):
                        sp.dma_start(dst[:, b, 0:NCH - 1, :],
                                     b_rows[pl, b, 0:(NCH - 1) * P, :].rearrange("(c p) d -> p c d", p=P)).then_inc(b_in, 16)
                        sp.dma_start(dst[0:HJ - (NCH - 1) * P, b, NCH - 1, :],
                                     b_rows[pl, b, (NCH - 1) * P:HJ, :]).then_inc(b_in, 16)

            for q in range(4):
                load_w(q)
            for s in range(A_FIRST, A_LAST):
                if on(s, -2):
                    load_x(s + 2, s % 2)
                if s == 0:
                    b_store()
                if s >= 0:
                    for q in (4 + 2 * s, 5 + 2 * s):
                        if q < 4 * EARLY:
                            load_w(q)
                if on(s, LAG_G):
                    store(s - LAG_G, (s - LAG_G) % 2)
                if on(s, 1):
                    load_xr(s - 1, (s - 1) % 2)
            for q in range(4 * EARLY, 4 * E9):
                load_w(q)
            for k in range(2):
                sp.wait_ge(s_out[k], 16 * (NF // 2))
            sp.dma_start(out, acc[0:T, :]).then_inc(done, 16)
            sp.wait_ge(done, 16)

        @block.tensor
        def _(pe):
            def kv(w, n):
                for m in range(INNER // P):
                    g = n * 8 + m
                    at_least(pe, kv_ev, g - 1)
                    for k in range(KD):
                        mm = pe.matmul(ps[:, g % 2, 0:B * J], w[:, k, m * P:(m + 1) * P], ctx_sb[:, k, :],
                                       start=(k == 0), stop=(k == KD - 1))
                    mm.then_inc(kv_mm, 1)

            pe.wait_ge(ctx_in, 16)
            pe.wait_ge(wk_in, 16)
            kv(wk_sb, 0)
            pe.wait_ge(wq_in, 16)
            for h in range(HEADS):
                r, m = (h % 2) * DH, h // 2
                at_least(pe, kv_ev, m + 1)
                at_least(pe, a_lo_ok, h - 1)
                for k in range(KD):
                    mm = pe.matmul(ps[:, 2 + h % 2, k * B * J:(k + 1) * B * J], wq_sb[r:r + DH, m, k * P:(k + 1) * P],
                                   kt_sb[r:r + DH, m, :], start=(k == 0), stop=(k == KD - 1), skip_group_check=True)
                mm.then_inc(a_mm, 1)
            pe.wait_ge(wv_in, 16)
            kv(wv_sb, 1)
            pe.wait_ge(wo_in, 16)
            for h in range(HEADS):
                r, m = (h % 2) * DH, h // 2
                at_least(pe, kv_ev, 8 + m + 1)
                at_least(pe, b_lo_ok, h - 1)
                for b in range(B):
                    mm = pe.matmul(ps[0:J, 4 + h % 2, b * D:(b + 1) * D], vt_sb[r:r + DH, m, b * J:(b + 1) * J],
                                   wo_sb[r:r + DH, m, :], start=(b == 0), stop=(b == B - 1), skip_group_check=True)
                mm.then_inc(b_mm, 1)

            def norm_turn(i, par, s):
                pe.wait_ge(xn_ok, i + 1)
                at_least(pe, lg_ok, s - LAG_G)
                for k in range(KD):
                    mm = pe.transpose(ps[:, 7, k * P:(k + 1) * P], xnb[:, par, k * P:(k + 1) * P], con[:, C_ID:C_ID + P])
                mm.then_inc(xt_mm, 1)

            def scores(i, par, b):
                pe.wait_ge(xl_ok, i + 1)
                at_least(pe, sub_ok, i)
                h0 = 0
                for c, nh in enumerate(SC_H):
                    w = nh * J
                    dst = ps[:, c, 0:w]
                    pe.matmul(dst.rearrange("p (h j) -> p h j", j=J), idb[:],
                              maskb[:, i, :].unsqueeze(1).to_broadcast([P, nh, J]), start=True, stop=False)
                    for k in range(KD):
                        for lhs, rhs in ((x_h, a_hi), (x_h, a_lo), (x_l, a_hi)):
                            mm = pe.matmul(dst, lhs[:, par, k, :], rhs[:, k, b, h0 * J:h0 * J + w], start=False,
                                           stop=(k == KD - 1 and lhs is x_l))
                    h0 += nh
                mm.then_inc(sc_mm, 1)

            def prob_turn(i, par):
                pe.wait_ge(norm_ok, i + 1)
                for g, c0 in enumerate((0, 4, 8)):
                    at_least(pe, ph_ok, 3 * i + g - 2)
                    at_least(pe, pl_ok, 3 * i + g - 2)
                    for c in range(c0, min(c0 + 4, NCH)):
                        mm = pe.transpose(ps[:, 3 + g, (c % 4) * P:(c % 4 + 1) * P], ebuf[par][:, c * P:(c + 1) * P],
                                          con[:, C_ID:C_ID + P])
                    mm.then_inc(pt_mm, 1)

            def project(i, b):
                at_least(pe, x1_ok, i)
                for c in range(NCH):
                    if c % 4 == 0:
                        pe.wait_ge(pl_ok, 3 * i + c // 4 + 1)
                    for n, (lhs, rhs) in enumerate(((pt_h, b_hi), (pt_h, b_lo), (pt_l, b_hi))):
                        mm = pe.matmul(ps[:, 6, 0:D], lhs[:, c, :], rhs[:, b, c, :],
                                       start=(c == 0 and n == 0), stop=(c == NCH - 1 and n == 2))
                mm.then_inc(out_mm, 1)

            def gate_turn(i, par, s):
                pe.wait_ge(xn2_ok, i + 1)
                at_least(pe, lg_ok, i)
                pe.wait_ge(xl_ok, cap(s + 2))
                pe.wait_ge(xh_ok, cap(s + 2))
                for k in range(KD):
                    mm = pe.transpose(ps[:, 7, k * P:(k + 1) * P], xn2b[:, par, k * P:(k + 1) * P], con[:, C_ID:C_ID + P])
                mm.then_inc(xn2t_mm, 1)

            def gate_logits(i, par):
                pe.wait_ge(xn2t_ok, i + 1)
                for k in range(KD):
                    mm = pe.matmul(ps[:, 7, D:D + E9], xn2t[:, par, k, :], gate_sb[:, k, :],
                                   start=(k == 0), stop=(k == KD - 1))
                mm.then_inc(gate_mm, 1)

            def step(s, n):
                if on(n, LAG_OUT):
                    prob_turn(s - LAG_OUT, (n - LAG_OUT) % 2)
                if on(n, -1):
                    norm_turn(s + 1, (n + 1) % 2, s)
                if on(n, 0):
                    scores(s, n % 2, s // TPB)
                if on(n, LAG_G):
                    gate_turn(s - LAG_G, (n - LAG_G) % 2, s)
                if on(n, LAG_OUT):
                    project(s - LAG_OUT, (s - LAG_OUT) // TPB)
                if on(n, LAG_G):
                    gate_logits(s - LAG_G, (n - LAG_G) % 2)

            pe.wait_ge(con_in, 16)
            pe.wait_ge(setup, 1)
            pe.wait_ge(mask_ok, 1)
            pe.wait_ge(a_lo_ok, HEADS)
            pe.wait_ge(bc_in, 48)
            pe.wait_ge(b_hi_ok, HEADS)
            pe.wait_ge(b_lo_ok, HEADS)
            for s in range(A_FIRST, A_LAST):
                if s == LAG_OUT:
                    pe.wait_ge(b_in, 16 * 8)
                step(s, s)

            pe.wait_ge(s16_ok, 1)
            s16 = R["s16"]
            rank = ps[:, 0, 0:(NT + 1) * E9]
            pe.matmul(rank, trib[:], s16.rearrange("p i e -> p (i e)"), start=True, stop=False, skip_group_check=True)
            for i in range(NT):
                w = NT - i
                mm = pe.matmul(rank[:, (i + 1) * E9:].rearrange("p (i e) -> p i e", e=E9), onesb[:],
                               s16[:, i, :].unsqueeze(1).to_broadcast([P, w, E9]), start=False, stop=(i == NT - 1),
                               skip_group_check=True)
            mm.then_inc(rank_mm, 1)
            pe.wait_ge(u_ok, 1)
            for q in range(2 * NT):
                pe.wait_ge(v_ok, q + 1)
                mm = pe.matmul(ps[:, 1, 0:3 * NF], vhot[:, q, :], R["u"][:, q].rearrange("p v t -> p (v t)"),
                               start=(q == 0), stop=(q == 2 * NT - 1))
            mm.then_inc(map_mm, 1)

            def f_turn(t, par):
                pe.wait_ge(g_in[par], (t // 2) * 16 + 16)
                at_least(pe, fxl_ok, t)
                for k in range(KD):
                    mm = pe.transpose(ps[:, 6, k * P:(k + 1) * P], xg[:, par, k * P:(k + 1) * P], con[:, C_ID:C_ID + P])
                mm.then_inc(fxt_mm, 1)

            def weights(off, n):
                return w_all[:, bass.ds(off, n)]

            def up(t, par, wbase):
                pe.wait_ge(fxl_ok, t + 1)
                half = HID // 2
                for c in range(4):
                    if c < 2:
                        at_least(pe, silu_ok, 2 * t + (c - 1))
                    else:
                        at_least(pe, h_ok, 2 * t + (c - 3))
                    for k in range(KD):
                        for lhs, pl in ((fx_h, 0), (fx_h, 1), (fx_l, 0)):
                            off = pl * WC + k * 2 * HID + c * half
                            mm = pe.matmul(ps[:, c, 0:half], lhs[:, par, k, :], weights(wbase + off, half),
                                           start=(k == 0 and lhs is fx_h and pl == 0), stop=(k == KD - 1 and lhs is fx_l))
                    mm.then_inc(w13_mm, 1)

            def h_turn(t, par):
                pe.wait_ge(h_ok, 2 * t + 2)
                for g, c0 in enumerate((0, 4)):
                    at_least(pe, fhl_ok, 2 * t + (g - 1))
                    for c in range(c0, min(c0 + 4, HC)):
                        mm = pe.transpose(ps[:, 4 + g, (c % 4) * P:(c % 4 + 1) * P], hb[:, par, c * P:(c + 1) * P],
                                          con[:, C_ID:C_ID + P])
                    mm.then_inc(fht_mm, 1)

            def down(t, wbase):
                at_least(pe, y_ok, t)
                for c in range(HC):
                    if c % 4 == 0:
                        pe.wait_ge(fhl_ok, 2 * t + c // 4 + 1)
                    for n, (lhs, pl) in enumerate(((ht_h, 0), (ht_h, 1), (ht_l, 0))):
                        mm = pe.matmul(ps[:, 7, 0:D], lhs[:, c, :], weights(wbase + (pl * WC + W13C + c * D), D),
                                       start=(c == 0 and n == 0), stop=(c == HC - 1 and n == 2))
                mm.then_inc(w2_mm, 1)

            pe.wait_ge(route_ok, 1)
            pe.wait_ge(w_hi_ok, 4 * E9)
            pe.wait_ge(w_lo_ok, 4 * E9)
            pe.wait_ge(hpad_ok, 1)

            def expert_base(t):
                return pe.value_load(eid[0:1, t:t + 1] if isinstance(t, int) else eid[0:1, bass.ds(t, 1)],
                                     min_val=0, max_val=E9 - 1) * (2 * WC)

            def fstep(s, n):
                if onf(n, 1):
                    h_turn(s - 1, (n - 1) % 2)
                if onf(n, -1):
                    f_turn(s + 1, (n + 1) % 2)
                if onf(n, 0):
                    up(s, n % 2, expert_base(s))
                if onf(n, 1):
                    down(s - 1, expert_base(s - 1))

            pipe_f(pe, fstep)

        @block.scalar
        def _(act):
            for h in range(HEADS):
                act.wait_ge(a_mm, h + 1)
                act.activation(a_hi[:, :, :, h * J:(h + 1) * J],
                               ps[:, 2 + h % 2, 0:KD * B * J].rearrange("p (k b j) -> p k b j", k=KD, b=B),
                               ACT.Copy).then_inc(a_hi_ok, 1)
            for h in range(HEADS):
                act.wait_ge(b_mm, h + 1)
                act.activation(bs_h[0:J, :, h, :], ps[0:J, 4 + h % 2, 0:B * D].rearrange("p (b d) -> p b d", b=B),
                               ACT.Copy, scale=SP_B).then_inc(b_hi_ok, 1)

            def w_high(q):
                act.wait_ge(w_in[q % 4], 16 * (q // 4 + 1))
                act.activation(stage[:, q % 4, :], stage[:, q % 4, :], ACT.Copy, scale=SP_W).then_inc(w_sc_ok, 1)
                act.wait_ge(w_sc_ok, q + 1)
                act.activation(w_chunk(q, 0), stage[:, q % 4, :], ACT.Copy).then_inc(w_hi_ok, 1)

            def x_high(i, par):
                act.wait_ge(xt_mm, i + 1)
                at_least(act, sc_mm, i - 1)
                act.activation(x_h[:, par], ps[:, 7, 0:D].rearrange("p (k t) -> p k t", k=KD), ACT.Copy).then_inc(xh_ok, 1)

            def exp(i, par):
                act.wait_ge(sub_ok, i + 1)
                act.activation(ebuf[par][:, 0:HJ], ebuf[par][:, 0:HJ], ACT.Exp, scale=DH ** -0.5).then_inc(exp_ok, 1)

            def p_high(i):
                at_least(act, out_mm, i)
                for g, (c0, c1) in enumerate(((0, 4), (4, 8), (8, 10))):
                    act.wait_ge(pt_mm, 3 * i + g + 1)
                    act.activation(pt_h[:, c0:c1, :], ps[:, 3 + g, 0:(c1 - c0) * P].rearrange("p (c t) -> p c t", t=P),
                                   ACT.Copy, scale=SP_P).then_inc(ph_ok, 1)

            def gate_copy(i, par):
                act.wait_ge(xn2t_mm, i + 1)
                at_least(act, gate_mm, i - 1)
                act.activation(xn2t[:, par], ps[:, 7, 0:D].rearrange("p (k t) -> p k t", k=KD), ACT.Copy).then_inc(xn2t_ok, 1)

            for s in range(A_FIRST, A_LAST):
                if on(s, LAG_OUT):
                    p_high(s - LAG_OUT)
                if on(s, -1):
                    x_high(s + 1, (s + 1) % 2)
                if on(s, LAG_G):
                    gate_copy(s - LAG_G, (s - LAG_G) % 2)
                if s >= -1:
                    if s == -1:
                        act.wait_ge(stat1_ok, 1)
                    if s == 0:
                        act.wait_ge(b_out, 16 * 4)
                    for q in (2 + 2 * s, 3 + 2 * s):
                        if q < 4 * EARLY:
                            w_high(q)
                if on(s, 0):
                    exp(s, s % 2)

            act.wait_ge(m_ok, 1)
            act.activation(R["sgm"], R["m"], ACT.Sigmoid).then_inc(sig_ok, 1)
            act.wait_ge(out_mm, NT)
            act.wait_ge(pt_mm, 3 * NT)
            act.wait_ge(sc_mm, NT)
            for q in range(4 * EARLY, 4 * E9):
                w_high(q)

            def fx_high(t, par):
                act.wait_ge(fxt_mm, t + 1)
                at_least(act, w13_mm, 4 * (t - 1))
                act.activation(fx_h[:, par], ps[:, 6, 0:D].rearrange("p (k t) -> p k t", k=KD), ACT.Copy).then_inc(fxh_ok, 1)

            def silu(t, par):
                at_least(act, h_ok, 2 * (t - 1))
                for c in range(2):
                    act.wait_ge(w13_mm, 4 * t + c + 1)
                    act.activation(sg[:, par, c * HID // 2:(c + 1) * HID // 2], ps[:, c, 0:HID // 2], ACT.Silu,
                                   scale=1.0 / SP_W).then_inc(silu_ok, 1)

            def fh_high(t):
                at_least(act, w2_mm, t)
                for g, (c0, c1) in enumerate(((0, 4), (4, 6))):
                    act.wait_ge(fht_mm, 2 * t + g + 1)
                    act.activation(ht_h[:, c0:c1, :], ps[:, 4 + g, 0:(c1 - c0) * P].rearrange("p (c t) -> p c t", t=P),
                                   ACT.Copy).then_inc(fhh_ok, 1)

            def fstep(s, n):
                if onf(n, 1):
                    fh_high(s - 1)
                if onf(n, -1):
                    fx_high(s + 1, (n + 1) % 2)
                if onf(n, 0):
                    silu(s, n % 2)

            act.wait_ge(route_ok, 1)
            pipe_f(act, fstep)

        @block.vector
        def _(dve):
            dve.memset(onesb[:], 1.0)
            dve.memset(xnb[:, 0], 0.0).then_inc(zero_ok, 1)
            dve.memset(ebuf[0][:, HJ:HJP], 0.0)
            dve.memset(ebuf[1][:, HJ:HJP], 0.0)
            dve.memset(mhalf[:], -0.5)
            dve.memset(b_hi[64:P, :, NCH - 1, :], 0.0)
            dve.memset(b_lo[64:P, :, NCH - 1, :], 0.0).then_inc(cpy, 1)
            dve.wait_ge(con_in, 16)
            dve.tensor_copy(idb[:], con[:, C_ID:C_ID + P])
            dve.tensor_copy(trib[:], con[:, C_TRI:C_TRI + P])
            dve.tensor_copy(iota16[:], con[:, C_IOTA:C_IOTA + P]).then_inc(setup, 1)

            def kv_copy(n, dst):
                for m in range(INNER // P):
                    g = n * 8 + m
                    dve.wait_ge(kv_mm, g + 1)
                    dve.tensor_copy(dst[:, m, :], ps[:, g % 2, 0:B * J]).then_inc(kv_ev, 1)

            kv_copy(0, kt_sb)
            for h in range(HEADS):
                dve.wait_ge(a_hi_ok, h + 1)
                src = ps[:, 2 + h % 2, 0:KD * B * J].rearrange("p (k b j) -> p k b j", k=KD, b=B)
                for k in range(KD):
                    ins = dve.tensor_tensor(a_lo[:, k, :, h * J:(h + 1) * J], src[:, k],
                                            a_hi[:, k, :, h * J:(h + 1) * J], ALU.subtract)
                ins.then_inc(a_lo_ok, 1)
            kv_copy(1, vt_sb)
            dve.wait_ge(xall_in, 16)
            st_all = ebuf[1]
            for i in range(NT):
                dve.bn_stats(st_all[:, i * 6:(i + 1) * 6], x_all[:, i, :]).then_inc(stats1, 1)
            for i in range(NT):
                dve.wait_ge(stats1, i + 1)
                ins = dve.bn_aggr(mv_all[:, i, :], st_all[:, i * 6:(i + 1) * 6])
            ins.then_inc(stat1_ok, 1)
            dve.wait_ge(mask_in, 16)
            dve.tensor_scalar(maskb, mask8, MASKED, None, ALU.mult).then_inc(mask_ok, 1)
            for h in range(HEADS):
                dve.wait_ge(b_hi_ok, h + 1)
                dve.scalar_tensor_tensor(out=bs_l[0:J, :, h, :], in0=ps[0:J, 4 + h % 2, 0:B * D].rearrange("p (b d) -> p b d", b=B),
                                         scalar=SP_B, in1=bs_h[0:J, :, h, :], op0=ALU.mult,
                                         op1=ALU.subtract).then_inc(b_lo_ok, 1)

            def normalise(i, par):
                dve.wait_ge(x_in[par], (i // 2) * 16 + 16)
                at_least(dve, xt_mm, i - 1)
                col = slice(i, i + 1) if isinstance(i, int) else bass.ds(i, 1)
                dve.tensor_scalar(xnb[:, par], xbuf[:, par], mv_all[:, col, 0], rstd_all[:, col], ALU.subtract,
                                  ALU.mult).then_inc(xn_ok, 1)

            def x_low(i, par):
                dve.wait_ge(xh_ok, i + 1)
                dve.tensor_tensor(x_l[:, par], ps[:, 7, 0:D].rearrange("p (k t) -> p k t", k=KD), x_h[:, par],
                                  ALU.subtract).then_inc(xl_ok, 1)

            def shift(i, par):
                dve.wait_ge(sc_mm, i + 1)
                h0 = 0
                srcs = []
                for c, nh in enumerate(SC_H):
                    srcs.append((h0, nh, ps[:, c, 0:nh * J].rearrange("p (h j) -> p h j", j=J)))
                    h0 += nh
                for h0, nh, src in srcs:
                    dve.tensor_reduce(mx[:, par, h0:h0 + nh], src, AX.X, ALU.max).then_inc(max_ok, 1)
                at_least(dve, pt_mm, 3 * (i - 1))
                for n, (h0, nh, src) in enumerate(srcs):
                    dve.wait_ge(max_ok, 3 * i + n + 1)
                    ins = dve.tensor_tensor(ebuf[par][:, h0 * J:(h0 + nh) * J].rearrange("p (h j) -> p h j", j=J), src,
                                            mx[:, par, h0:h0 + nh].unsqueeze(2).to_broadcast([P, nh, J]), ALU.subtract)
                ins.then_inc(sub_ok, 1)

            def sums(i, par):
                dve.wait_ge(exp_ok, i + 1)
                dve.tensor_reduce(rs[:, par], ebuf[par][:, 0:HJ].rearrange("p (h j) -> p h j", j=J), AX.X,
                                  ALU.add).then_inc(sum_ok, 1)
                dve.wait_ge(sum_ok, i + 1)
                at_least(dve, norm_ok, i - 1)
                dve.reciprocal(rr[:, par], rs[:, par]).then_inc(rec_ok, 1)

            def p_low(i):
                for g, (c0, c1) in enumerate(((0, 4), (4, 8), (8, 10))):
                    dve.wait_ge(ph_ok, 3 * i + g + 1)
                    dve.scalar_tensor_tensor(out=pt_l[:, c0:c1, :],
                                             in0=ps[:, 3 + g, 0:(c1 - c0) * P].rearrange("p (c t) -> p c t", t=P),
                                             scalar=SP_P, in1=pt_h[:, c0:c1, :], op0=ALU.mult,
                                             op1=ALU.subtract).then_inc(pl_ok, 1)

            def residual(i, par):
                dve.wait_ge(out_mm, i + 1)
                dve.wait_ge(xb_ok, i + 1)
                at_least(dve, x1_out[par], (i // 2) * 16)
                at_least(dve, xn2_ok, i - 1)
                dve.scalar_tensor_tensor(out=x1b[:, par], in0=ps[:, 6, 0:D], scalar=1.0 / (SP_P * SP_B), in1=xbuf2(par),
                                         op0=ALU.mult, op1=ALU.add).then_inc(x1_ok, 1)

            def xbuf2(par):
                return xrb[:, par]

            def stats(i, par):
                dve.wait_ge(x1_ok, i + 1)
                dve.bn_stats(st6[:, par], x1b[:, par]).then_inc(st_ok, 1)

            def aggregate(i, par):
                dve.wait_ge(st_ok, i + 1)
                at_least(dve, xn2_ok, i - 1)
                at_least(dve, rstd_ok, i - 1)
                dve.bn_aggr(mv2[:, par], st6[:, par]).then_inc(mv_ok, 1)

            def normalise2(i, par):
                dve.wait_ge(rstd_ok, i + 1)
                at_least(dve, xn2_out[par], (i // 2) * 16)
                at_least(dve, xn2t_mm, i - 1)
                dve.tensor_scalar(xn2b[:, par], x1b[:, par], mv2[:, par, 0:1], rstd2[:, par], ALU.subtract,
                                  ALU.mult).then_inc(xn2_ok, 1)

            def logits(i):
                dve.wait_ge(gate_mm, i + 1)
                row = lg[:, i, :] if isinstance(i, int) else lg[:, bass.ds(i, 1), :]
                dve.tensor_tensor(row, ps[:, 7, D:D + E9], gb_b[:], ALU.add).then_inc(lg_ok, 1)

            def step(s, n):
                if on(n, LAG_X1):
                    residual(s - LAG_X1, (n - LAG_X1) % 2)
                if on(n, LAG_OUT):
                    p_low(s - LAG_OUT)
                if on(n, LAG_X1):
                    stats(s - LAG_X1, (n - LAG_X1) % 2)
                if on(n, -1):
                    x_low(s + 1, (n + 1) % 2)
                if on(n, LAG_X1):
                    aggregate(s - LAG_X1, (n - LAG_X1) % 2)
                if on(n, 1):
                    sums(s - 1, (n - 1) % 2)
                if on(n, -2):
                    normalise(s + 2, n % 2)
                if on(n, 0):
                    shift(s, n % 2)
                if on(n, LAG_XN2):
                    normalise2(s - LAG_XN2, (n - LAG_XN2) % 2)
                if on(n, LAG_G):
                    logits(s - LAG_G)

            dve.wait_ge(rstd1, 2)
            dve.wait_ge(bc_in, 48)
            dve.wait_ge(zero_out, 32)
            for s in range(A_FIRST, A_LAST):
                step(s, s)

            count = [0]

            def link(ins):
                count[0] += 1
                ins.then_inc(rt, 1)
                dve.wait_ge(rt, count[0])

            r = R
            rev = con[:, C_REV:C_REV + E9].unsqueeze(1).to_broadcast([P, NT, E9])

            def rows(a):
                return a.unsqueeze(2).to_broadcast([P, NT, E9])

            dve.wait_ge(lg_ok, NT)
            dve.wait_ge(xn2_out[0], 16 * NT // 2)
            dve.wait_ge(xn2_out[1], 16 * NT // 2)
            dve.wait_ge(x1_out[0], 16 * NT // 2)
            dve.wait_ge(x1_out[1], 16 * NT // 2)
            dve.wait_ge(w_lo_ok, 4 * EARLY)
            link(dve.tensor_scalar(lg[:], lg[:], Z_ONE, None, ALU.min))
            link(dve.tensor_reduce(r["m"][:, 0], lg[:], AX.X, ALU.max))
            for k, (src, oh) in enumerate(((lg[:], r["oh1"]), (r["lg2"], r["oh2"]))):
                if k:
                    link(dve.scalar_tensor_tensor(out=r["lg2"], in0=r["oh1"], scalar=MASKED, in1=lg[:], op0=ALU.mult,
                                                  op1=ALU.add))
                    ins = dve.tensor_reduce(r["m"][:, 1], r["lg2"], AX.X, ALU.max)
                    link(ins)
                link(dve.tensor_tensor(r["eq"], src, rows(r["m"][:, k]), ALU.is_ge))
                link(dve.tensor_tensor(r["eq"], r["eq"], rev, ALU.mult))
                link(dve.tensor_reduce(r["c"][:, k], r["eq"], AX.X, ALU.max))
                link(dve.tensor_tensor(oh, rev, rows(r["c"][:, k]), ALU.is_equal))
            dve.memset(r["s16"][:, NT, :], 0.0)
            dve.tensor_tensor(r["s16"][:, 0:NT, :], r["oh1"], r["oh2"], ALU.add).then_inc(s16_ok, 1)
            dve.tensor_copy(r["cws"][:, 0:1], r["m"][:, 0, 0:1]).then_inc(m_ok, 1)
            dve.wait_ge(sig_ok, 1)
            link(dve.tensor_tensor(r["wsum"], r["sgm"][:, 0], r["sgm"][:, 1], ALU.add))
            link(dve.tensor_scalar(r["wsum"], r["wsum"], 1e-20, None, ALU.add))
            link(dve.reciprocal(r["wrec"], r["wsum"]))
            link(dve.tensor_tensor(r["cwv"], r["sgm"], r["wrec"].unsqueeze(1).to_broadcast([P, 2, NT]), ALU.mult))
            u1 = r["ueq"][:, 0:1, 0:2 * NT].rearrange("p a q -> p (a q)")
            link(dve.tensor_copy(u1, r["cwv"].rearrange("p k i -> p (k i)")))
            dve.tensor_copy(r["val"][:, 1], u1)
            link(dve.tensor_tensor(r["val"][:, 2], r["cwv"].rearrange("p k i -> p (k i)"), u1, ALU.subtract))
            for k in range(2):
                ins = dve.tensor_copy(r["val"][:, 0, k * NT:(k + 1) * NT], con[:, C_TOK:C_TOK + NT])
            link(ins)
            dve.wait_ge(rank_mm, 1)
            rank = ps[:, 0, 0:(NT + 1) * E9].rearrange("p (i e) -> p i e", e=E9)
            link(dve.tensor_scalar(r["cnti"][:, 0:E9], rank[:, NT, :], float(P - 1), None, ALU.add))
            link(dve.tensor_scalar(r["cnti"][:, 0:E9], r["cnti"][:, 0:E9], 7, None, ALU.logical_shift_right))
            link(dve.tensor_copy(r["ntl"][:, 0:E9], r["cnti"][:, 0:E9]))
            link(dve.tensor_tensor(r["cmul"], con[:, C_LT:C_LT + E9 * E9].rearrange("p (a b) -> p a b", b=E9),
                                   r["ntl"][:, 0:E9].unsqueeze(1).to_broadcast([P, E9, E9]), ALU.mult))
            link(dve.tensor_reduce(r["cin"][:, 0:E9], r["cmul"], AX.X, ALU.add))
            link(dve.tensor_tensor(r["cex"][:, 0:E9], r["cin"][:, 0:E9], r["ntl"][:, 0:E9], ALU.subtract))
            link(dve.scalar_tensor_tensor(out=r["slot"], in0=r["cex"][:, 0:E9].unsqueeze(1).to_broadcast([P, NT, E9]),
                                          scalar=float(P), in1=rank[:, 0:NT, :], op0=ALU.mult, op1=ALU.add))
            for k, oh in enumerate((r["oh1"], r["oh2"])):
                link(dve.tensor_tensor(r["sel"], r["slot"], oh, ALU.mult))
                link(dve.tensor_reduce(r["sl"][:, k], r["sel"], AX.X, ALU.add))
            link(dve.tensor_copy(r["sli"], r["sl"]))
            dve.tensor_scalar(r["pi"], r["sli"], P - 1, None, ALU.bitwise_and)
            link(dve.tensor_scalar(r["ti"], r["sli"], 7, None, ALU.logical_shift_right))
            dve.tensor_copy(r["pf"], r["pi"].rearrange("p k i -> p (k i)"))
            link(dve.tensor_copy(r["tf"], r["ti"].rearrange("p k i -> p (k i)")))
            link(dve.tensor_tensor(r["ueq"], r["tf"].unsqueeze(2).to_broadcast([P, 2 * NT, NF]),
                                   con[:, C_IOTA:C_IOTA + NF].unsqueeze(1).to_broadcast([P, 2 * NT, NF]), ALU.is_equal))
            for v in range(3):
                ins = dve.tensor_tensor(r["u"][:, :, v, :], r["ueq"], r["val"][:, v].unsqueeze(2).to_broadcast([P, 2 * NT, NF]),
                                        ALU.mult)
            ins.then_inc(u_ok, 1)
            for q in range(2 * NT):
                dve.tensor_scalar(vhot[:, q, :], iota16[:], r["pf"][:, q:q + 1], None, ALU.is_equal).then_inc(v_ok, 1)
            link(dve.tensor_tensor(r["ecmp"], con[:, C_IOTA:C_IOTA + NF].unsqueeze(2).to_broadcast([P, NF, E9]),
                                   r["cin"][:, 0:E9].unsqueeze(1).to_broadcast([P, NF, E9]), ALU.is_ge))
            link(dve.tensor_reduce(r["ef"], r["ecmp"], AX.X, ALU.add))
            link(dve.tensor_scalar(eid[:], r["ef"], float(E9 - 1), None, ALU.min))
            dve.wait_ge(map_mm, 1)
            tab = ps[:, 1, 0:3 * NF].rearrange("p (v t) -> p v t", v=3)
            link(dve.tensor_scalar(r["pad"], tab[:, 0], 0.0, None, ALU.is_equal))
            link(dve.tensor_scalar(r["pad"], r["pad"], con[:, C_P:C_P + 1], None, ALU.mult))
            link(dve.tensor_scalar(r["idf"], tab[:, 0], float(T), None, ALU.add))
            link(dve.tensor_tensor(idx_all[:], r["idf"], r["pad"], ALU.add))
            link(dve.tensor_copy(r["cws"], tab[:, 1]))
            link(dve.tensor_tensor(r["cws"], tab[:, 2], r["cws"], ALU.add))
            link(dve.tensor_scalar(cw_all[:], r["cws"], 1.0 / SP_W, None, ALU.mult))
            for k in range(2):
                ins = dve.memset(hb[:, k, HID:HC * P], 0.0)
            link(ins)
            dve.sem_inc(hpad_ok, 1)
            dve.sem_inc(route_ok, 1)

            def fx_low(t, par):
                dve.wait_ge(fxh_ok, t + 1)
                dve.tensor_tensor(fx_l[:, par], ps[:, 6, 0:D].rearrange("p (k t) -> p k t", k=KD), fx_h[:, par],
                                  ALU.subtract).then_inc(fxl_ok, 1)

            def hidden(t, par):
                at_least(dve, fht_mm, 2 * (t - 1))
                for c in range(2):
                    dve.wait_ge(silu_ok, 2 * t + c + 1)
                    dve.wait_ge(w13_mm, 4 * t + c + 3)
                    dve.scalar_tensor_tensor(out=hb[:, par, c * HID // 2:(c + 1) * HID // 2], in0=ps[:, 2 + c, 0:HID // 2],
                                             scalar=1.0 / SP_W, in1=sg[:, par, c * HID // 2:(c + 1) * HID // 2],
                                             op0=ALU.mult, op1=ALU.mult).then_inc(h_ok, 1)

            def fh_low(t):
                for g, (c0, c1) in enumerate(((0, 4), (4, 6))):
                    dve.wait_ge(fhh_ok, 2 * t + g + 1)
                    dve.tensor_tensor(ht_l[:, c0:c1, :], ps[:, 4 + g, 0:(c1 - c0) * P].rearrange("p (c t) -> p c t", t=P),
                                      ht_h[:, c0:c1, :], ALU.subtract).then_inc(fhl_ok, 1)

            def weigh(t, par):
                dve.wait_ge(w2_mm, t + 1)
                at_least(dve, s_out[par], (t // 2) * 16)
                col = slice(t, t + 1) if isinstance(t, int) else bass.ds(t, 1)
                dve.tensor_scalar(yb[:, par], ps[:, 7, 0:D], cw_all[:, col], None, ALU.mult).then_inc(y_ok, 1)

            def fstep(s, n):
                if onf(n, 1):
                    fh_low(s - 1)
                if onf(n, -1):
                    fx_low(s + 1, (n + 1) % 2)
                if onf(n, 2):
                    weigh(s - 2, n % 2)
                if onf(n, 0):
                    hidden(s, n % 2)

            pipe_f(dve, fstep)

        @block.gpsimd
        def _(pool):
            pool.wait_ge(stat1_ok, 1)
            pool.wait_ge(cpy, 1)
            pool.tensor_scalar(rstd_all[:], mv_all[:, :, 1], LN_EPS, None, ALU.add).then_inc(rstd1, 1)
            pool.wait_ge(rstd1, 1)
            pool.tensor_tensor(rstd_all[:], rstd_all[:], mhalf[:], ALU.pow).then_inc(rstd1, 1)
            pool.wait_ge(bc_in, 48)

            def w_low(q):
                pool.wait_ge(w_hi_ok, q + 1)
                pool.tensor_tensor(w_chunk(q, 1), stage[:, q % 4, :], w_chunk(q, 0), ALU.subtract).then_inc(w_lo_ok, 1)

            def norm(i, par):
                pool.wait_ge(rec_ok, i + 1)
                e3 = ebuf[par][:, 0:HJ].rearrange("p (h j) -> p h j", j=J)
                pool.tensor_tensor(e3, e3, rr[:, par].unsqueeze(2).to_broadcast([P, HEADS, J]), ALU.mult).then_inc(norm_ok, 1)

            def bias(i, par):
                pool.wait_ge(xr_in[par], (i // 2) * 16 + 16)
                pool.tensor_tensor(xrb[:, par], xrb[:, par], bo_b[:], ALU.add).then_inc(xb_ok, 1)

            def rstd(i, par):
                pool.wait_ge(mv_ok, i + 1)
                pool.tensor_scalar(ve2[:, par], mv2[:, par, 1:2], LN_EPS, None, ALU.add).then_inc(ve_ok, 1)
                pool.wait_ge(ve_ok, i + 1)
                pool.tensor_tensor(rstd2[:, par], ve2[:, par], mhalf[:, 0:1], ALU.pow).then_inc(rstd_ok, 1)

            def step(s, n):
                if on(n, 2):
                    bias(s - 2, n % 2)
                if 0 <= 2 + 2 * n < 4 * EARLY:
                    w_low(2 + 2 * n)
                if on(n, LAG_X1):
                    rstd(s - LAG_X1, (n - LAG_X1) % 2)
                if on(n, 1):
                    norm(s - 1, (n - 1) % 2)
                if 0 <= 3 + 2 * n < 4 * EARLY:
                    w_low(3 + 2 * n)

            for s in range(A_FIRST, A_LAST):
                step(s, s)
            for q in range(4 * EARLY, 4 * E9):
                w_low(q)
            pool.wait_ge(route_ok, 1)
            pool.wait_ge(zero_out, 32)

            def gather(t, par):
                at_least(pool, g_in[par], (t // 2) * 16)
                at_least(pool, fxt_mm, t - 1)
                col = slice(t, t + 1) if isinstance(t, int) else bass.ds(t, 1)
                pool.tensor_copy(idg[:, par], idx_all[:, col]).then_inc(idg_ok, 1)
                pool.wait_ge(idg_ok, t + 1)
                pool.sem_inc(dma_go, 1)
                pool.indirect_dma_start(out=xg[:, par], out_offset=None, in_=xn2_rows,
                                        in_offset=bass.IndirectOffsetOnAxis(ap=idg[:, par], axis=0)).then_inc(g_in[par], 16)

            def scatter(t, par):
                at_least(pool, s_out[par], (t // 2) * 16)
                col = slice(t, t + 1) if isinstance(t, int) else bass.ds(t, 1)
                pool.tensor_copy(ids[:, par], idx_all[:, col]).then_inc(ids_ok, 1)
                pool.wait_ge(ids_ok, t + 1)
                pool.wait_ge(y_ok, t + 1)
                at_least(pool, s_out[1 - par], ((t + 1) // 2) * 16)
                pool.sem_inc(dma_go, 1)
                pool.indirect_dma_start(out=acc, out_offset=bass.IndirectOffsetOnAxis(ap=ids[:, par], axis=0), in_=yb[:, par],
                                        in_offset=None, compute_op=ALU.add).then_inc(s_out[par], 16)

            def fstep(s, n):
                if onf(n, 3):
                    scatter(s - 3, (n - 3) % 2)
                if onf(n, -2):
                    gather(s + 2, n % 2)

            pipe_f(pool, fstep)


def shape_constants():
    c = np.zeros((P, C_ALL), np.float32)
    p = np.arange(P)
    c[:, C_ID:C_ID + P] = np.eye(P)
    c[:, C_TRI:C_TRI + P] = p[:, None] < p[None, :]
    c[:, C_IOTA:C_IOTA + P] = p[None, :]
    c[:, C_REV:C_REV + E9] = E9 - np.arange(E9)
    c[:, C_LT:C_LT + E9 * E9] = (np.arange(E9)[None, :] <= np.arange(E9)[:, None]).reshape(-1)
    c[:, C_TOK:C_TOK + NT] = np.arange(NT)[None, :] * P + p[:, None] - T
    c[:, C_P] = p
    return c


def kernel(**inputs):
    import concourse.bacc as bacc
    from concourse.bass_utils import run_bass_kernel_spmd

    a = {k: np.asarray(v) for k, v in inputs.items()}
    w1 = np.concatenate([a["L0_ffn_w1"], a["L0_ffn_new_w1"]])
    w2 = np.concatenate([a["L0_ffn_w2"], a["L0_ffn_new_w2"]])
    w3 = np.concatenate([a["L0_ffn_w3"], a["L0_ffn_new_w3"]])
    w13 = np.concatenate([w1, w3], axis=1).reshape(E9, 2 * HID, KD, P).transpose(0, 3, 2, 1).reshape(E9, P, W13C)
    w2t = np.concatenate([w2.transpose(0, 2, 1), np.zeros((E9, HC * P - HID, D), np.float32)], axis=1)
    w2t = w2t.reshape(E9, HC, P, D).transpose(0, 2, 1, 3).reshape(E9, P, HC * D)
    arrays = {
        "x": a["x"].reshape(T, D),
        "ctxT": a["ctx_1024"].reshape(B * J, D).T,
        "mask": np.ascontiguousarray(a["mask_BxSxS2_bk1"].reshape(NT, P, J).transpose(1, 0, 2)).reshape(P, NT * J).view(np.uint32),
        "wq": a["L0_xattn_Wq"].T,
        "wk": a["L0_xattn_Wk"],
        "wv": a["L0_xattn_Wv"],
        "wo": a["L0_xattn_Wo"],
        "bo": a["L0_xattn_bo"],
        "wt": np.concatenate([w13, w2t], axis=2),
        "gate": np.concatenate([a["L0_ffn_gate_weight"], a["L0_ffn_new_gate_weight"]]).T,
        "gbias": np.concatenate([np.zeros(E9 - 1, np.float32), a["L0_ffn_gate_bias"]]),
        "consts": shape_constants(),
    }
    nc = bacc.Bacc("TRN2", target_bir_lowering=False, num_devices=1)
    ins, args = {}, []
    for name, v in arrays.items():
        v = np.ascontiguousarray(v)
        ins["in_" + name] = v
        args.append(nc.dram_tensor("in_" + name, v.shape, mybir.dt.from_np(v.dtype), kind="ExternalInput").ap())
    out = nc.dram_tensor("out_rows", (T, D), F32, kind="ExternalOutput").ap()
    build(nc, *args, out)
    r = run_bass_kernel_spmd(nc, [ins], core_ids=[0])
    return r.results[0]["out_rows"].reshape(B, N, D)
```

```python
from contextlib import ExitStack

import numpy as np

import concourse.bass as bass
from concourse import mybir

F32, F16, BF16 = mybir.dt.float32, mybir.dt.float16, mybir.dt.bfloat16
I32, U32, U8 = mybir.dt.int32, mybir.dt.uint32, mybir.dt.uint8
ALU = mybir.AluOpType
ACT = mybir.ActivationFunctionType
AX = mybir.AxisListType

P = 128
B, N, D = 2, 1024, 256
T = B * N
J = 77
HEADS, DH = 16, 64
INNER = HEADS * DH
HJ = HEADS * J
HJP = 1280
NCH = HJP // P
KD = D // P
E9 = 9
HID = 704
HC = 6
NT = T // P
TPB = NT // B
NF = (2 * T - E9) // P + E9
TR = T + P
W13C = KD * 2 * HID
WC = W13C + HC * D
EARLY = 6
QC = WC // 4
SC_H = [6, 6, 4]
LN_EPS = 1e-5
SP_P, SP_B, SP_W = 1024.0, 64.0, 64.0
MASKED = -3.0e38
Z_ONE = 16.635532
C_ID, C_TRI, C_IOTA, C_REV, C_LT, C_TOK, C_P = 0, 128, 256, 384, 393, 474, 490
C_ALL = 491


def at_least(eng, sem, n):
    if isinstance(n, int) and n <= 0:
        return
    eng.wait_ge(sem, n)


def pipeline(eng, step, first, last, lo, hi):
    for s in range(first, lo):
        step(s, s)
    with eng.Fori(0, (hi - lo) // 2) as j:
        for u in range(2):
            step(j * 2 + (lo + u), lo + u)
    for s in range(hi, last):
        step(s, s)


def build(nc, x, ctxT, mask, wq, wk, wv, wo, bo, wt, gate, gbias, consts, out):
    with ExitStack() as ctx:
        def sb(name, shape, dt):
            return ctx.enter_context(nc.sbuf_tensor(name, shape, dt))

        def sem(name):
            return ctx.enter_context(nc.semaphore(name))

        def sems(name, n):
            return [sem(f"{name}{k}") for k in range(n)]

        acc = out
        xn2_rows = nc.dram_tensor("xn2_rows", [TR, D], F32, kind="Internal").ap()
        b_rows = nc.dram_tensor("b_rows", [2, B, HJ, D], F16, kind="Internal").ap()

        w_all = sb("w_all", [P, E9 * 2 * WC], F16)
        con = sb("con", [P, C_ALL], F32)
        idb = sb("idb", [P, P], BF16)
        trib = sb("trib", [P, P], BF16)
        onesb = sb("onesb", [P, P], BF16)
        iota16 = sb("iota16", [P, P], F16)
        bo_b = sb("bo_b", [P, D], F32)
        gb_b = sb("gb_b", [P, E9], F32)
        gate_sb = sb("gate_sb", [P, KD, E9], F32)
        mv_all = sb("mv_all", [P, NT, 2], F32)
        rstd_all = sb("rstd_all", [P, NT], F32)
        mhalf = sb("mhalf", [P, NT], F32)
        eps = sb("eps", [P, 1], F32)
        lg = sb("lg", [P, NT, E9], F32)
        idx_all = sb("idx_all", [P, NF], U32)
        cw_all = sb("cw_all", [P, NF], F32)
        eid = sb("eid", [P, NF], I32)
        stage = sb("stage", [P, 4, QC], F32)
        WORK = 28000
        work = sb("work", [P, WORK], mybir.dt.uint8)
        ps = ctx.enter_context(nc.psum_tensor("ps", [P, 8, 512], F32))

        def view(base, off, shape, dt):
            n = int(np.prod(shape)) * mybir.dt.size(dt)
            v = base[:, off:off + n].bitcast(dt)
            names = "abcd"[:len(shape)]
            if len(shape) > 1:
                v = v.rearrange(f"p ({' '.join(names)}) -> p {' '.join(names)}", **dict(zip(names[1:], shape[1:])))
            return v, off + n

        LATE = EARLY * 2 * WC
        late = w_all[:, LATE:]

        def lview(off, shape, dt):
            n = int(np.prod(shape)) * mybir.dt.size(dt)
            v = late[:, off // 2:(off + n) // 2].bitcast(dt)
            names = "abcd"[:len(shape)]
            if len(shape) > 1:
                v = v.rearrange(f"p ({' '.join(names)}) -> p {' '.join(names)}", **dict(zip(names[1:], shape[1:])))
            return v, off + n

        o = 0
        a_hi, o = lview(o, [KD, B, HJ], F16)
        a_lo, o = lview(o, [KD, B, HJ], F16)
        b_hi, o = lview(o, [B, NCH, D], F16)
        b_lo, o = lview(o, [B, NCH, D], F16)
        maskb, o = lview(o, [NT, J], BF16)
        mask32, o = lview(o, [NT * J // 4], U32)
        mask8 = mask32.bitcast(U8).rearrange("p (i j) -> p i j", j=J)
        ebuf0, o = lview(o, [HJP], F32)
        x_h, o = lview(o, [2, KD, P], F16)
        x_l, o = lview(o, [2, KD, P], F16)
        assert o <= 3 * 2 * WC * 2, o
        o = 0
        ebuf1, o = view(work, o, [HJP], F32)
        pt_h, o = view(work, o, [NCH, P], F16)
        pt_l, o = view(work, o, [NCH, P], F16)
        xbuf, o = view(work, o, [2, D], F32)
        xrb, o = view(work, o, [2, D], F32)
        xnb, o = view(work, o, [2, D], F32)
        x1b, o = view(work, o, [2, D], F32)
        xn2b, o = view(work, o, [2, D], F32)
        xn2t, o = view(work, o, [2, KD, P], F32)
        mx, o = view(work, o, [2, HEADS], F32)
        rs, o = view(work, o, [2, HEADS], F32)
        rr, o = view(work, o, [2, HEADS], F32)
        st6, o = view(work, o, [2, 6], F32)
        mv2, o = view(work, o, [2, 2], F32)
        ve2, o = view(work, o, [2, 1], F32)
        rstd2, o = view(work, o, [2, 1], F32)
        assert o <= WORK, o
        ebuf = [ebuf0, ebuf1]
        a_hi_f, a_lo_f = (a.rearrange("p k b n -> p (k b n)") for a in (a_hi, a_lo))
        b_hi_f, b_lo_f = (a.rearrange("p b c d -> p (b c d)") for a in (b_hi, b_lo))
        maskf = maskb.rearrange("p i j -> p (i j)")
        o = 0
        xg, o = view(work, o, [2, D], F32)
        fx_h, o = view(work, o, [2, KD, P], F16)
        fx_l, o = view(work, o, [2, KD, P], F16)
        sg, o = view(work, o, [2, HID], F32)
        hb, o = view(work, o, [2, HC * P], F32)
        ht_h, o = view(work, o, [HC, P], F16)
        ht_l, o = view(work, o, [HC, P], F16)
        yb, o = view(work, o, [2, D], F32)
        idg, o = view(work, o, [2, 1], U32)
        ids, o = view(work, o, [2, 1], U32)
        assert o <= WORK, o
        pro = w_all[:, 2 * WC:LATE]

        def pview(off, shape, dt):
            n = int(np.prod(shape)) * mybir.dt.size(dt)
            v = pro[:, off // 2:(off + n) // 2].bitcast(dt)
            names = "abcd"[:len(shape)]
            if len(shape) > 1:
                v = v.rearrange(f"p ({' '.join(names)}) -> p {' '.join(names)}", **dict(zip(names[1:], shape[1:])))
            return v, off + n

        o = 0
        wq_sb, o = pview(o, [INNER // P, D], F32)
        wk_sb, o = pview(o, [KD, INNER], F32)
        wv_sb, o = pview(o, [KD, INNER], F32)
        wo_sb, o = pview(o, [INNER // P, D], F32)
        ctx_sb, o = pview(o, [KD, B * J], F32)
        kvt_h, o = pview(o, [4 * INNER // P, B * J], F16)
        kvt_l, o = pview(o, [4 * INNER // P, B * J], F16)
        kvt_h4, kvt_l4 = (a.rearrange("p (g r) j -> p g r j", r=2) for a in (kvt_h, kvt_l))
        bs_h, o = pview(o, [B, HEADS, D], F16)
        bs_l, o = pview(o, [B, HEADS, D], F16)
        assert o <= 5 * 2 * WC * 2, o
        qo_split = stage[:].rearrange("p q c -> p (q c)").bitcast(F16)[:, 0:4 * 8 * D].rearrange(
            "p (a m d) -> p a m d", a=4, d=D)
        wq_h, wq_l, wo_h, wo_l = (qo_split[:, k] for k in range(4))
        x_all = w_all[:, 0:NT * D * 2].bitcast(F32).rearrange("p (i d) -> p i d", d=D)
        R = {}
        o = 0
        for name, shape, dt in [
            ("m", [2, NT], F32), ("sgm", [2, NT], F32), ("c", [2, NT], F32), ("wsum", [NT], F32), ("wrec", [NT], F32),
            ("cwv", [2, NT], F32), ("eq", [NT, E9], F32), ("oh1", [NT, E9], F32), ("oh2", [NT, E9], F32),
            ("lg2", [NT, E9], F32), ("s16", [NT + 1, E9], BF16), ("cnt", [E9 + 1], F32), ("cnti", [E9 + 1], I32),
            ("ntl", [E9 + 1], F32), ("cmul", [E9, E9], F32), ("cin", [E9 + 1], F32), ("cex", [E9 + 1], F32),
            ("slot", [NT, E9], F32), ("sel", [NT, E9], F32), ("sl", [2, NT], F32), ("sli", [2, NT], I32),
            ("pi", [2, NT], I32), ("ti", [2, NT], I32), ("pf", [2 * NT], F32), ("tf", [2 * NT], F16),
            ("val", [3, 2 * NT], F16), ("ueq", [2 * NT, NF], F16), ("u", [2 * NT, 3, NF], F16),
            ("pad", [NF], F32), ("idf", [NF], F32), ("idf2", [NF], F32), ("cws", [NF], F32), ("ecmp", [NF, E9], F32),
            ("ef", [NF], F32), ("vhot", [2 * NT, P], F16),
        ]:
            if name == "val":
                o = (o + 3) // 4 * 4
            R[name], o = view(work, o, shape, dt)
            o = (o + 3) // 4 * 4
        assert o <= WORK, o
        vhot = R["vhot"]

        con_in, bc_in, ctx_in, wk_in, wq_in, wv_in, wo_in, mask_in = (sem(n) for n in (
            "con_in", "bc_in", "ctx_in", "wk_in", "wq_in", "wv_in", "wo_in", "mask_in"))
        xall_in = sem("xall_in")
        setup = sem("setup")
        cpy = sem("cpy")
        mask_ok = sem("mask_ok")
        stats1, stat1_ok, rstd1 = sem("stats1"), sem("stat1_ok"), sem("rstd1")
        kv_zero, kv_mm, kv_hi_ok, kv_lo_ok = sem("kv_zero"), sem("kv_mm"), sem("kv_hi_ok"), sem("kv_lo_ok")
        wq_hi_ok, wq_lo_ok, wo_sc_ok, wo_hi_ok, wo_lo_ok = (sem(n) for n in (
            "wq_hi_ok", "wq_lo_ok", "wo_sc_ok", "wo_hi_ok", "wo_lo_ok"))
        a_mm, a_hi_ok, a_lo_ok = sem("a_mm"), sem("a_hi_ok"), sem("a_lo_ok")
        b_mm, b_hi_ok, b_lo_ok = sem("b_mm"), sem("b_hi_ok"), sem("b_lo_ok")
        b_out, b_in = sems("b_out", B), sems("b_in", B)
        w_in = sems("w_in", 4)
        w_sc_ok, w_hi_ok, w_lo_ok = sem("w_sc_ok"), sem("w_hi_ok"), sem("w_lo_ok")
        x_in, xr_in = sems("x_in", 2), sems("xr_in", 2)
        x1_out, xn2_out = sems("x1_out", 2), sems("xn2_out", 2)
        xn_ok, xt_mm, xh_ok, xl_ok, sc_mm = (sem(n) for n in ("xn_ok", "xt_mm", "xh_ok", "xl_ok", "sc_mm"))
        max_ok, sub_ok, exp_ok, sum_ok, rec_ok, norm_ok = (sem(n) for n in (
            "max_ok", "sub_ok", "exp_ok", "sum_ok", "rec_ok", "norm_ok"))
        pt_mm, ph_ok, pl_ok, out_mm, xb_ok, x1_ok = (sem(n) for n in ("pt_mm", "ph_ok", "pl_ok", "out_mm", "xb_ok", "x1_ok"))
        st_ok, mv_ok, ve_ok, rstd_ok, xn2_ok = (sem(n) for n in ("st_ok", "mv_ok", "ve_ok", "rstd_ok", "xn2_ok"))
        xn2t_mm, xn2t_ok, gate_mm, lg_ok = (sem(n) for n in ("xn2t_mm", "xn2t_ok", "gate_mm", "lg_ok"))
        rt = sem("rt")
        s16_ok, rank_mm, sig_ok, m_ok, v_ok, ueq_ok, u_ok, map_mm, idx_ok, route_ok = (sem(n) for n in (
            "s16_ok", "rank_mm", "sig_ok", "m_ok", "v_ok", "ueq_ok", "u_ok", "map_mm", "idx_ok", "route_ok"))
        zero_ok, zero_out = sem("zero_ok"), sem("zero_out")
        g_in, s_out = sems("g_in", 2), sems("s_out", 2)
        idg_ok, ids_ok, hpad_ok = sem("idg_ok"), sem("ids_ok"), sem("hpad_ok")
        fxt_mm, fxh_ok, fxl_ok, w13_mm, silu_ok, h_ok = (sem(n) for n in (
            "fxt_mm", "fxh_ok", "fxl_ok", "w13_mm", "silu_ok", "h_ok"))
        fht_mm, fhh_ok, fhl_ok, w2_mm, y_ok = (sem(n) for n in ("fht_mm", "fhh_ok", "fhl_ok", "w2_mm", "y_ok"))
        dma_go, aggr_go = sem("dma_go"), sem("aggr_go")

        xv = x.rearrange("(i p) d -> i p d", p=P)
        LAG_OUT, LAG_X1, LAG_XN2, LAG_G = 2, 3, 4, 5
        A_FIRST, A_LAST = -2, NT + LAG_G + 1
        A_LO, A_HI, W_STEP = 6, 14, 3

        def on(s, lag):
            return 0 <= s - lag < NT

        def prologue_steps(step):
            for s in range(A_FIRST, 0):
                step(s, s)

        def pipe_a(eng, step):
            pipeline(eng, step, 0, A_LAST, A_LO, A_HI)

        def cap(n):
            return min(n, NT) if isinstance(n, int) else n

        F_FIRST, F_LAST, F_LO, F_HI = -2, NF + 4, 6, NF - 2

        def onf(s, lag):
            return 0 <= s - lag < NF

        def pipe_f(eng, step):
            pipeline(eng, step, F_FIRST, F_LAST, F_LO, F_HI)

        LATE_LOAD = W_STEP + 2 * EARLY - 1
        LATE_SPLIT = NT + 2
        U_AT = 2
        def on_w(n):
            return W_STEP <= n < W_STEP + 2 * EARLY

        def chunk_parts(n):
            return (0, 1) if (n - W_STEP) % 2 == 0 else (2, 3)

        def w_chunk(e, part, plane):
            off = plane * WC + part * QC
            if isinstance(e, int):
                return w_all[:, e * 2 * WC + off:e * 2 * WC + off + QC]
            return w_all[:, bass.ds(e * (2 * WC) + off, QC)]

        PRO_BANKS, B_BANKS = (0, 1, 6, 7), (0, 1, 6, 3)
        STATS_A = 11
        B_SPLIT = 12

        block = ctx.enter_context(nc.Block())

        @block.sync
        def _(sp):
            sp.dma_start(con[:], consts).then_inc(con_in, 16)
            sp.dma_start(ctx_sb, ctxT.rearrange("(k p) j -> p k j", p=P)).then_inc(ctx_in, 16)
            sp.dma_start(wk_sb, wk.rearrange("(k p) n -> p k n", p=P)).then_inc(wk_in, 16)
            sp.dma_start(wv_sb, wv.rearrange("(k p) n -> p k n", p=P)).then_inc(wv_in, 16)
            sp.dma_start(wq_sb, wq.rearrange("(m p) n -> p m n", p=P)).then_inc(wq_in, 16)
            sp.dma_start(mask32, mask).then_inc(mask_in, 16)
            sp.dma_start(wo_sb, wo.rearrange("(m p) n -> p m n", p=P)).then_inc(wo_in, 16)
            sp.dma_start(x_all, x.rearrange("(i p) d -> p i d", p=P)).then_inc(xall_in, 16)
            sp.dma_start(bo_b[:], bo.partition_broadcast(P)).then_inc(bc_in, 16)
            sp.dma_start(gb_b[:], gbias.partition_broadcast(P)).then_inc(bc_in, 16)
            sp.dma_start(gate_sb[:], gate.rearrange("(k p) e -> p k e", p=P)).then_inc(bc_in, 16)
            sp.wait_ge(zero_ok, 1)
            sp.dma_start(acc[T:TR, :], xnb[:, 0]).then_inc(zero_out, 16)
            sp.dma_start(xn2_rows[T:TR, :], xnb[:, 0]).then_inc(zero_out, 16)

            def load_w(e, part, used=None):
                at_least(sp, w_lo_ok, (4 * e if used is None else used) + (part - 3))
                src = wt[e, :, part * QC:(part + 1) * QC] if isinstance(e, int) else \
                    wt[bass.ds(e, 1), :, part * QC:(part + 1) * QC].rearrange("e p c -> (e p) c")
                sp.dma_start(stage[:, part, :], src).then_inc(w_in[part], 16)

            def load_x(i, par):
                at_least(sp, xn_ok, i - 1)
                sp.dma_start(xbuf[:, par], xv[i]if isinstance(i, int) else x[bass.ds(i * P, P), :]).then_inc(x_in[par], 16)

            def load_xr(i, par):
                at_least(sp, x1_ok, i - 1)
                sp.dma_start(xrb[:, par], xv[i]if isinstance(i, int) else x[bass.ds(i * P, P), :]).then_inc(xr_in[par], 16)

            def store(i, par):
                rows = slice(i * P, (i + 1) * P) if isinstance(i, int) else bass.ds(i * P, P)
                at_least(sp, x1_ok, i + 1)
                sp.dma_start(acc[rows, :], x1b[:, par]).then_inc(x1_out[par], 16)
                at_least(sp, xn2_ok, i + 1)
                sp.dma_start(xn2_rows[rows, :], xn2b[:, par]).then_inc(xn2_out[par], 16)

            def b_store(b, g):
                hs = slice(g * HEADS // 2, (g + 1) * HEADS // 2)
                for pl, src in enumerate((bs_h, bs_l)):
                    sp.dma_start(b_rows[pl, b].rearrange("(h j) d -> j h d", j=J)[:, hs], src[0:J, b, hs]).then_inc(b_out[b], 16)

            def b_load(b):
                sp.wait_ge(b_out[b], 16 * 4)
                for pl, dst in enumerate((b_hi, b_lo)):
                    sp.dma_start(dst[:, b, 0:NCH - 1, :],
                                 b_rows[pl, b, 0:(NCH - 1) * P, :].rearrange("(c p) d -> p c d", p=P)).then_inc(b_in[b], 16)
                    sp.dma_start(dst[0:HJ - (NCH - 1) * P, b, NCH - 1, :],
                                 b_rows[pl, b, (NCH - 1) * P:HJ, :]).then_inc(b_in[b], 16)

            def step(s, n):
                if n == 1:
                    b_load(0)
                if on(n, -2):
                    load_x(s + 2, n % 2)
                if n == 1:
                    b_load(1)
                if on(n, LAG_G):
                    store(s - LAG_G, (n - LAG_G) % 2)
                if on(n, 1):
                    load_xr(s - 1, (n - 1) % 2)
                if on_w(n + 1):
                    for part in chunk_parts(n + 1):
                        load_w((s + 1 - W_STEP) // 2, part, 2 * (s + 1 - W_STEP - (n + 1 - W_STEP) % 2))
                if n in (LATE_LOAD, LATE_LOAD + 1):
                    for part in chunk_parts(n + 1):
                        load_w(EARLY, part)

            prologue_steps(step)
            for g in range(2):
                sp.wait_ge(b_lo_ok, (g + 1) * HEADS // 2)
                for b in range(B):
                    b_store(b, g)
            pipe_a(sp, step)
            for e in range(EARLY + 1, E9):
                for part in range(4):
                    load_w(e, part)
            for k in range(2):
                sp.wait_ge(s_out[k], 16 * (NF // 2))

        @block.tensor
        def _(pe):
            def kv(w, n):
                for m in range(INNER // P):
                    g = n * 8 + m
                    at_least(pe, kv_lo_ok, g - 3)
                    for k in range(KD):
                        mm = pe.matmul(ps[:, PRO_BANKS[g % 4], 0:B * J], w[:, k, m * P:(m + 1) * P], ctx_sb[:, k, :],
                                       start=(k == 0), stop=(k == KD - 1))
                    mm.then_inc(kv_mm, 1)

            pe.wait_ge(ctx_in, 16)
            pe.wait_ge(wk_in, 16)
            kv(wk_sb, 0)
            pe.wait_ge(wv_in, 16)
            kv(wv_sb, 1)
            pe.wait_ge(kv_zero, 1)
            for h in range(HEADS):
                m = h // 2
                if h == 0:
                    pe.wait_ge(kv_lo_ok, 8)
                pe.wait_ge(wq_lo_ok, m // 4 + 1)
                at_least(pe, a_lo_ok, h - 3)
                for k in range(KD):
                    for n, (lhs, rhs) in enumerate(((wq_h, kvt_h4), (wq_h, kvt_l4), (wq_l, kvt_h4))):
                        mm = pe.matmul(ps[:, 2 + h % 4, k * B * J:(k + 1) * B * J], lhs[:, m, k * P:(k + 1) * P],
                                       rhs[:, m, h % 2, :], start=(k == 0 and n == 0), stop=(k == KD - 1 and n == 2),
                                       skip_group_check=True)
                mm.then_inc(a_mm, 1)

            def make_b(h0, h1):
                for h in range(h0, h1):
                    m = h // 2
                    at_least(pe, b_lo_ok, h - 3)
                    for b in range(B):
                        for n, (lhs, rhs) in enumerate(((kvt_h4, wo_h), (kvt_l4, wo_h), (kvt_h4, wo_l))):
                            mm = pe.matmul(ps[0:J, B_BANKS[h % 4], b * D:(b + 1) * D], lhs[:, INNER // P + m, h % 2, b * J:(b + 1) * J],
                                           rhs[:, m, :], start=(b == 0 and n == 0), stop=(b == B - 1 and n == 2),
                                           skip_group_check=True)
                    mm.then_inc(b_mm, 1)

            pe.wait_ge(kv_lo_ok, 16)
            pe.wait_ge(wo_lo_ok, 1)
            pe.wait_ge(a_lo_ok, HEADS)
            make_b(0, B_SPLIT)

            def norm_turn(i, par, s):
                pe.wait_ge(xn_ok, i + 1)
                at_least(pe, lg_ok, s - LAG_G)
                for k in range(KD):
                    mm = pe.transpose(ps[:, 7, k * P:(k + 1) * P], xnb[:, par, k * P:(k + 1) * P], con[:, C_ID:C_ID + P])
                mm.then_inc(xt_mm, 1)

            def scores(i, par, b):
                pe.wait_ge(xl_ok, i + 1)
                h0 = 0
                for c, nh in enumerate(SC_H):
                    at_least(pe, sub_ok, 3 * i + (c - 2))
                    w = nh * J
                    dst = ps[:, c, 0:w]
                    pe.matmul(dst.rearrange("p (h j) -> p h j", j=J), idb[:],
                              maskf[:, bass.ds(i * J, J)].unsqueeze(1).to_broadcast([P, nh, J]), start=True, stop=False)
                    for k in range(KD):
                        for lhs, rhs in ((x_h, a_hi_f), (x_l, a_hi_f), (x_h, a_lo_f)):
                            mm = pe.matmul(dst, lhs[:, par, k, :], rhs[:, bass.ds(b * HJ + (k * B * HJ + h0 * J), w)], start=False,
                                           stop=(k == KD - 1 and rhs is a_lo_f))
                    mm.then_inc(sc_mm, 1)
                    h0 += nh

            def prob_turn(i, par):
                pe.wait_ge(norm_ok, i + 1)
                for g, c0 in enumerate((0, 4, 8)):
                    at_least(pe, ph_ok, 3 * i + g - 2)
                    at_least(pe, pl_ok, 3 * i + g - 2)
                    for c in range(c0, min(c0 + 4, NCH)):
                        mm = pe.transpose(ps[:, 3 + g, (c % 4) * P:(c % 4 + 1) * P], ebuf[par][:, c * P:(c + 1) * P],
                                          con[:, C_ID:C_ID + P])
                    mm.then_inc(pt_mm, 1)

            def project(i, b):
                at_least(pe, x1_ok, i)
                for c in range(NCH):
                    if c % 4 == 0:
                        pe.wait_ge(pl_ok, 3 * i + c // 4 + 1)
                    for n, (lhs, rhs) in enumerate(((pt_h, b_hi_f), (pt_l, b_hi_f), (pt_h, b_lo_f))):
                        mm = pe.matmul(ps[:, 6, 0:D], lhs[:, c, :], rhs[:, bass.ds(b * (NCH * D) + c * D, D)],
                                       start=(c == 0 and n == 0), stop=(c == NCH - 1 and n == 2))
                mm.then_inc(out_mm, 1)

            def gate_turn(i, par, s):
                pe.wait_ge(xn2_ok, i + 1)
                at_least(pe, lg_ok, i)
                pe.wait_ge(xl_ok, cap(s + 2))
                pe.wait_ge(xh_ok, cap(s + 2))
                for k in range(KD):
                    mm = pe.transpose(ps[:, 7, k * P:(k + 1) * P], xn2b[:, par, k * P:(k + 1) * P], con[:, C_ID:C_ID + P])
                mm.then_inc(xn2t_mm, 1)

            def gate_logits(i, par):
                pe.wait_ge(xn2t_ok, i + 1)
                for k in range(KD):
                    mm = pe.matmul(ps[:, 7, D:D + E9], xn2t[:, par, k, :], gate_sb[:, k, :],
                                   start=(k == 0), stop=(k == KD - 1))
                mm.then_inc(gate_mm, 1)

            def step(s, n):
                if n == LAG_OUT:
                    pe.wait_ge(b_in[0], 16 * 4)
                if n == A_LO - 1:
                    pe.wait_ge(b_in[1], 16 * 4)
                if on(n, LAG_OUT):
                    prob_turn(s - LAG_OUT, (n - LAG_OUT) % 2)
                if on(n, -1):
                    norm_turn(s + 1, (n + 1) % 2, s)
                if on(n, 0):
                    scores(s, n % 2, s // TPB)
                if on(n, LAG_G):
                    gate_turn(s - LAG_G, (n - LAG_G) % 2, s)
                if on(n, LAG_OUT):
                    project(s - LAG_OUT, (s - LAG_OUT) // TPB)
                if on(n, LAG_G):
                    gate_logits(s - LAG_G, (n - LAG_G) % 2)

            pe.wait_ge(con_in, 16)
            prologue_steps(step)
            make_b(B_SPLIT, HEADS)
            pe.wait_ge(setup, 1)
            pe.wait_ge(mask_ok, 1)
            pe.wait_ge(bc_in, 48)
            pe.wait_ge(b_hi_ok, HEADS)
            pe.wait_ge(b_lo_ok, HEADS)
            pipe_a(pe, step)

            pe.wait_ge(s16_ok, 1)
            s16 = R["s16"]
            rank = ps[:, 0, 0:(NT + 1) * E9]
            pe.matmul(rank, trib[:], s16.rearrange("p i e -> p (i e)"), start=True, stop=False, skip_group_check=True)
            for i in range(NT):
                w = NT - i
                mm = pe.matmul(rank[:, (i + 1) * E9:].rearrange("p (i e) -> p i e", e=E9), onesb[:],
                               s16[:, i, :].unsqueeze(1).to_broadcast([P, w, E9]), start=False, stop=(i == NT - 1),
                               skip_group_check=True)
            mm.then_inc(rank_mm, 1)
            pe.wait_ge(u_ok, 2)
            for q in range(2 * NT):
                pe.wait_ge(v_ok, q + 1)
                mm = pe.matmul(ps[:, 1, 0:3 * NF], vhot[:, q, :], R["u"][:, q].rearrange("p v t -> p (v t)"),
                               start=(q == 0), stop=(q == 2 * NT - 1))
            mm.then_inc(map_mm, 1)

            def f_turn(t, par):
                pe.wait_ge(g_in[par], (t // 2) * 16 + 16)
                at_least(pe, fxl_ok, t)
                for k in range(KD):
                    mm = pe.transpose(ps[:, 6, k * P:(k + 1) * P], xg[:, par, k * P:(k + 1) * P], con[:, C_ID:C_ID + P])
                mm.then_inc(fxt_mm, 1)

            def weights(off, n):
                return w_all[:, bass.ds(off, n)]

            def up(t, par, wbase):
                pe.wait_ge(fxl_ok, t + 1)
                half = HID // 2
                for c in range(4):
                    if c < 2:
                        at_least(pe, silu_ok, 2 * t + (c - 1))
                    else:
                        at_least(pe, h_ok, 2 * t + (c - 3))
                    for k in range(KD):
                        for lhs, pl in ((fx_h, 0), (fx_l, 0), (fx_h, 1)):
                            off = pl * WC + k * 2 * HID + c * half
                            mm = pe.matmul(ps[:, c, 0:half], lhs[:, par, k, :], weights(wbase + off, half),
                                           start=(k == 0 and lhs is fx_h and pl == 0), stop=(k == KD - 1 and pl == 1))
                    mm.then_inc(w13_mm, 1)

            def h_turn(t, par):
                pe.wait_ge(h_ok, 2 * t + 2)
                for g, c0 in enumerate((0, 4)):
                    at_least(pe, fhl_ok, 2 * t + (g - 1))
                    for c in range(c0, min(c0 + 4, HC)):
                        mm = pe.transpose(ps[:, 4 + g, (c % 4) * P:(c % 4 + 1) * P], hb[:, par, c * P:(c + 1) * P],
                                          con[:, C_ID:C_ID + P])
                    mm.then_inc(fht_mm, 1)

            def down(t, wbase):
                at_least(pe, y_ok, t)
                for c in range(HC):
                    if c % 4 == 0:
                        pe.wait_ge(fhl_ok, 2 * t + c // 4 + 1)
                    for n, (lhs, pl) in enumerate(((ht_h, 0), (ht_l, 0), (ht_h, 1))):
                        mm = pe.matmul(ps[:, 7, 0:D], lhs[:, c, :], weights(wbase + (pl * WC + W13C + c * D), D),
                                       start=(c == 0 and n == 0), stop=(c == HC - 1 and n == 2))
                mm.then_inc(w2_mm, 1)

            pe.wait_ge(route_ok, 1)
            pe.wait_ge(hpad_ok, 1)

            def expert(t):
                return pe.value_load(eid[0:1, t:t + 1] if isinstance(t, int) else eid[0:1, bass.ds(t, 1)],
                                     min_val=0, max_val=E9 - 1)

            def fstep(s, n):
                if onf(n, 1):
                    h_turn(s - 1, (n - 1) % 2)
                if onf(n, -1):
                    f_turn(s + 1, (n + 1) % 2)
                if onf(n, 0):
                    e = expert(s)
                    if n < 5:
                        pe.wait_ge(w_lo_ok, e * 4 + 4)
                    elif n == 5:
                        pe.wait_ge(w_lo_ok, 4 * E9)
                    up(s, n % 2, e * (2 * WC))
                if onf(n, 1):
                    down(s - 1, expert(s - 1) * (2 * WC))

            pipe_f(pe, fstep)

        @block.scalar
        def _(act):
            def kv_high(g):
                act.wait_ge(kv_mm, g + 1)
                for r in range(2):
                    rows = slice(r * DH, (r + 1) * DH)
                    act.activation(kvt_h4[rows, g, r, :], ps[rows, PRO_BANKS[g % 4], 0:B * J], ACT.Copy).then_inc(kv_hi_ok, 1)

            def wq_high(g):
                act.wait_ge(wq_in, 16)
                act.activation(wq_h[:, 4 * g:4 * g + 4], wq_sb[:, 4 * g:4 * g + 4], ACT.Copy, scale=SP_W).then_inc(wq_hi_ok, 1)

            for g in range(12):
                kv_high(g)
            wq_high(0)
            for g in range(12, 16):
                kv_high(g)
            wq_high(1)
            act.wait_ge(wo_in, 16)
            act.activation(wo_sb, wo_sb, ACT.Copy, scale=SP_B).then_inc(wo_sc_ok, 1)
            for h in range(HEADS):
                if h == 4:
                    act.wait_ge(wo_sc_ok, 1)
                    act.activation(wo_h, wo_sb, ACT.Copy).then_inc(wo_hi_ok, 1)
                act.wait_ge(a_mm, h + 1)
                act.activation(a_hi[:, :, :, h * J:(h + 1) * J],
                               ps[:, 2 + h % 4, 0:KD * B * J].rearrange("p (k b j) -> p k b j", k=KD, b=B),
                               ACT.Copy, scale=1.0 / SP_W).then_inc(a_hi_ok, 1)

            def split_b(h0, h1):
                for h in range(h0, h1):
                    act.wait_ge(b_mm, h + 1)
                    act.activation(bs_h[0:J, :, h, :], ps[0:J, B_BANKS[h % 4], 0:B * D].rearrange("p (b d) -> p b d", b=B),
                                   ACT.Copy).then_inc(b_hi_ok, 1)

            split_b(0, B_SPLIT)

            def w_high(e, parts):
                for part in parts:
                    act.wait_ge(w_in[part], e * 16 + 16)
                    act.activation(stage[:, part, :], stage[:, part, :], ACT.Copy, scale=SP_W).then_inc(w_sc_ok, 1)
                for part in parts:
                    act.wait_ge(w_sc_ok, e * 4 + (part + 1))
                    act.activation(w_chunk(e, part, 0), stage[:, part, :], ACT.Copy).then_inc(w_hi_ok, 1)

            def x_high(i, par):
                act.wait_ge(xt_mm, i + 1)
                at_least(act, sc_mm, 3 * (i - 1))
                act.activation(x_h[:, par], ps[:, 7, 0:D].rearrange("p (k t) -> p k t", k=KD), ACT.Copy).then_inc(xh_ok, 1)

            def exp(i, par):
                act.wait_ge(sub_ok, 3 * i + 3)
                act.activation(ebuf[par][:, 0:HJ], ebuf[par][:, 0:HJ], ACT.Exp, scale=DH ** -0.5).then_inc(exp_ok, 1)

            def p_high(i):
                at_least(act, out_mm, i)
                for g, (c0, c1) in enumerate(((0, 4), (4, 8), (8, 10))):
                    act.wait_ge(pt_mm, 3 * i + g + 1)
                    act.activation(pt_h[:, c0:c1, :], ps[:, 3 + g, 0:(c1 - c0) * P].rearrange("p (c t) -> p c t", t=P),
                                   ACT.Copy, scale=SP_P).then_inc(ph_ok, 1)

            def gate_copy(i, par):
                act.wait_ge(xn2t_mm, i + 1)
                at_least(act, gate_mm, i - 1)
                act.activation(xn2t[:, par], ps[:, 7, 0:D].rearrange("p (k t) -> p k t", k=KD), ACT.Copy).then_inc(xn2t_ok, 1)

            def step(s, n):
                if on(n, LAG_OUT):
                    p_high(s - LAG_OUT)
                if on(n, -1):
                    x_high(s + 1, (n + 1) % 2)
                if n == W_STEP:
                    act.wait_ge(stat1_ok, 1)
                if n == W_STEP + 2:
                    for b in range(B):
                        act.wait_ge(b_out[b], 16 * 4)
                if on_w(n):
                    w_high((s - W_STEP) // 2, chunk_parts(n))
                if on(n, LAG_G):
                    gate_copy(s - LAG_G, (n - LAG_G) % 2)
                if on(n, 0):
                    exp(s, n % 2)
                if n == LATE_SPLIT:
                    act.wait_ge(out_mm, NT)
                    act.wait_ge(pt_mm, 3 * NT)
                    act.wait_ge(sc_mm, 3 * NT)
                if LATE_SPLIT <= n < LATE_SPLIT + 3:
                    w_high(EARLY, {0: (0,), 1: (1,), 2: (2, 3)}[n - LATE_SPLIT])

            prologue_steps(step)
            split_b(B_SPLIT, HEADS)
            pipe_a(act, step)
            act.wait_ge(m_ok, 1)
            act.activation(R["sgm"], R["m"], ACT.Sigmoid).then_inc(sig_ok, 1)
            for part in range(4):
                w_high(EARLY + 1, (part,))
            for part in range(4):
                act.wait_ge(w_in[part], (E9 - 1) * 16 + 16)
                act.activation(w_chunk(E9 - 1, part, 0), stage[:, part, :], ACT.Copy, scale=SP_W).then_inc(w_hi_ok, 1)

            def fx_high(t, par):
                act.wait_ge(fxt_mm, t + 1)
                at_least(act, w13_mm, 4 * (t - 1))
                act.activation(fx_h[:, par], ps[:, 6, 0:D].rearrange("p (k t) -> p k t", k=KD), ACT.Copy).then_inc(fxh_ok, 1)

            def silu(t, par):
                at_least(act, h_ok, 2 * (t - 1))
                for c in range(2):
                    act.wait_ge(w13_mm, 4 * t + c + 1)
                    act.activation(sg[:, par, c * HID // 2:(c + 1) * HID // 2], ps[:, c, 0:HID // 2], ACT.Silu,
                                   scale=1.0 / SP_W).then_inc(silu_ok, 1)

            def fh_high(t):
                at_least(act, w2_mm, t)
                for g, (c0, c1) in enumerate(((0, 4), (4, 6))):
                    act.wait_ge(fht_mm, 2 * t + g + 1)
                    act.activation(ht_h[:, c0:c1, :], ps[:, 4 + g, 0:(c1 - c0) * P].rearrange("p (c t) -> p c t", t=P),
                                   ACT.Copy).then_inc(fhh_ok, 1)

            def fstep(s, n):
                if onf(n, 1):
                    fh_high(s - 1)
                if onf(n, -1):
                    fx_high(s + 1, (n + 1) % 2)
                if onf(n, 0):
                    silu(s, n % 2)

            act.wait_ge(route_ok, 1)
            pipe_f(act, fstep)

        @block.vector
        def _(dve):
            dve.memset(onesb[:], 1.0)
            dve.memset(xnb[:, 0], 0.0).then_inc(zero_ok, 1)
            for a in (kvt_h4, kvt_l4):
                for r in range(2):
                    ins = dve.memset(a[r * DH:(r + 1) * DH, :, 1 - r, :].bitcast(F32), 0.0)
            ins.then_inc(kv_zero, 1)
            dve.memset(ebuf[0][:, HJ:HJP], 0.0)
            dve.memset(ebuf[1][:, HJ:HJP], 0.0)
            dve.memset(mhalf[:], -0.5)
            dve.memset(eps[:], LN_EPS)
            dve.memset(b_hi[64:P, :, NCH - 1, :], 0.0)
            dve.memset(b_lo[64:P, :, NCH - 1, :], 0.0).then_inc(cpy, 1)
            dve.wait_ge(con_in, 16)
            dve.tensor_copy(idb[:], con[:, C_ID:C_ID + P])
            dve.tensor_copy(trib[:], con[:, C_TRI:C_TRI + P])
            dve.tensor_copy(iota16[:], con[:, C_IOTA:C_IOTA + P]).then_inc(setup, 1)

            def kv_low(g):
                for r in range(2):
                    rows = slice(r * DH, (r + 1) * DH)
                    dve.wait_ge(kv_hi_ok, 2 * g + r + 1)
                    ins = dve.tensor_tensor(kvt_l4[rows, g, r, :], ps[rows, PRO_BANKS[g % 4], 0:B * J], kvt_h4[rows, g, r, :],
                                            ALU.subtract)
                ins.then_inc(kv_lo_ok, 1)

            def wq_low(g):
                dve.wait_ge(wq_hi_ok, g + 1)
                dve.scalar_tensor_tensor(out=wq_l[:, 4 * g:4 * g + 4], in0=wq_sb[:, 4 * g:4 * g + 4], scalar=SP_W,
                                         in1=wq_h[:, 4 * g:4 * g + 4], op0=ALU.mult, op1=ALU.subtract).then_inc(wq_lo_ok, 1)

            st_all = ebuf[1]

            def stats1_of(i):
                dve.bn_stats(st_all[:, i * 6:(i + 1) * 6], x_all[:, i, :]).then_inc(stats1, 1)

            for g in range(12):
                kv_low(g)
            wq_low(0)
            for g in range(12, 16):
                kv_low(g)
            wq_low(1)
            for h in range(HEADS):
                dve.wait_ge(a_hi_ok, h + 1)
                src = ps[:, 2 + h % 4, 0:KD * B * J].rearrange("p (k b j) -> p k b j", k=KD, b=B)
                ins = dve.scalar_tensor_tensor(out=a_lo[:, :, :, h * J:(h + 1) * J], in0=src, scalar=1.0 / SP_W,
                                               in1=a_hi[:, :, :, h * J:(h + 1) * J], op0=ALU.mult, op1=ALU.subtract)
                ins.then_inc(a_lo_ok, 1)
                if h == HEADS - STATS_A:
                    dve.wait_ge(xall_in, 16)
                if h >= HEADS - STATS_A:
                    stats1_of(h - (HEADS - STATS_A))

            def low_b(h0, h1):
                for h in range(h0, h1):
                    if h < NT - STATS_A:
                        stats1_of(STATS_A + h)
                    if h == NT - STATS_A:
                        for i in range(NT):
                            dve.wait_ge(stats1, i + 1)
                            ins = dve.bn_aggr(mv_all[:, i, :], st_all[:, i * 6:(i + 1) * 6])
                        ins.then_inc(stat1_ok, 1)
                    dve.wait_ge(b_hi_ok, h + 1)
                    dve.tensor_tensor(bs_l[0:J, :, h, :], ps[0:J, B_BANKS[h % 4], 0:B * D].rearrange("p (b d) -> p b d", b=B),
                                      bs_h[0:J, :, h, :], ALU.subtract).then_inc(b_lo_ok, 1)

            low_b(0, B_SPLIT - 2)

            def normalise(i, par):
                dve.wait_ge(x_in[par], (i // 2) * 16 + 16)
                at_least(dve, xt_mm, i - 1)
                col = slice(i, i + 1) if isinstance(i, int) else bass.ds(i, 1)
                dve.tensor_scalar(xnb[:, par], xbuf[:, par], mv_all[:, col, 0], rstd_all[:, col], ALU.subtract,
                                  ALU.mult).then_inc(xn_ok, 1)

            def x_low(i, par):
                dve.wait_ge(xh_ok, i + 1)
                dve.tensor_tensor(x_l[:, par], ps[:, 7, 0:D].rearrange("p (k t) -> p k t", k=KD), x_h[:, par],
                                  ALU.subtract).then_inc(xl_ok, 1)

            def score_banks():
                h0 = 0
                for c, nh in enumerate(SC_H):
                    yield h0, nh, ps[:, c, 0:nh * J].rearrange("p (h j) -> p h j", j=J)
                    h0 += nh

            def maxima(i, par):
                for c, (h0, nh, src) in enumerate(score_banks()):
                    dve.wait_ge(sc_mm, 3 * i + (c + 1))
                    dve.tensor_reduce(mx[:, par, h0:h0 + nh], src, AX.X, ALU.max).then_inc(max_ok, 1)

            def shift(i, par):
                at_least(dve, pt_mm, 3 * (i - 1))
                for c, (h0, nh, src) in enumerate(score_banks()):
                    dve.wait_ge(max_ok, 3 * i + (c + 1))
                    dve.tensor_tensor(ebuf[par][:, h0 * J:(h0 + nh) * J].rearrange("p (h j) -> p h j", j=J), src,
                                      mx[:, par, h0:h0 + nh].unsqueeze(2).to_broadcast([P, nh, J]),
                                      ALU.subtract).then_inc(sub_ok, 1)

            def sums(i, par):
                dve.wait_ge(exp_ok, i + 1)
                dve.tensor_reduce(rs[:, par], ebuf[par][:, 0:HJ].rearrange("p (h j) -> p h j", j=J), AX.X,
                                  ALU.add).then_inc(sum_ok, 1)
                dve.wait_ge(sum_ok, i + 1)
                at_least(dve, norm_ok, i - 1)
                dve.reciprocal(rr[:, par], rs[:, par]).then_inc(rec_ok, 1)

            def p_low(i):
                for g, (c0, c1) in enumerate(((0, 4), (4, 8), (8, 10))):
                    dve.wait_ge(ph_ok, 3 * i + g + 1)
                    dve.scalar_tensor_tensor(out=pt_l[:, c0:c1, :],
                                             in0=ps[:, 3 + g, 0:(c1 - c0) * P].rearrange("p (c t) -> p c t", t=P),
                                             scalar=SP_P, in1=pt_h[:, c0:c1, :], op0=ALU.mult,
                                             op1=ALU.subtract).then_inc(pl_ok, 1)

            def residual(i, par):
                dve.wait_ge(out_mm, i + 1)
                dve.wait_ge(xb_ok, i + 1)
                at_least(dve, x1_out[par], (i // 2) * 16)
                at_least(dve, xn2_ok, i - 1)
                dve.scalar_tensor_tensor(out=x1b[:, par], in0=ps[:, 6, 0:D], scalar=1.0 / (SP_P * SP_B), in1=xbuf2(par),
                                         op0=ALU.mult, op1=ALU.add).then_inc(x1_ok, 1)

            def xbuf2(par):
                return xrb[:, par]

            def stats(i, par):
                dve.wait_ge(x1_ok, i + 1)
                dve.bn_stats(st6[:, par], x1b[:, par]).then_inc(st_ok, 1)

            def aggregate(i, par):
                dve.wait_ge(st_ok, i + 1)
                at_least(dve, xn2_ok, i - 1)
                at_least(dve, rstd_ok, i - 1)
                dve.sem_inc(aggr_go, 1)
                dve.bn_aggr(mv2[:, par], st6[:, par]).then_inc(mv_ok, 1)

            def normalise2(i, par):
                dve.wait_ge(rstd_ok, i + 1)
                at_least(dve, xn2_out[par], (i // 2) * 16)
                at_least(dve, xn2t_mm, i - 1)
                dve.tensor_scalar(xn2b[:, par], x1b[:, par], mv2[:, par, 0:1], rstd2[:, par], ALU.subtract,
                                  ALU.mult).then_inc(xn2_ok, 1)

            def logits(i):
                dve.wait_ge(gate_mm, i + 1)
                row = lg[:, i, :] if isinstance(i, int) else lg[:, bass.ds(i, 1), :]
                dve.tensor_tensor(row, ps[:, 7, D:D + E9], gb_b[:], ALU.add).then_inc(lg_ok, 1)

            def step(s, n):
                if on(n, 1):
                    sums(s - 1, (n - 1) % 2)
                if on(n, LAG_OUT):
                    p_low(s - LAG_OUT)
                if on(n, -1):
                    x_low(s + 1, (n + 1) % 2)
                if on(n, LAG_X1):
                    residual(s - LAG_X1, (n - LAG_X1) % 2)
                if on(n, 0):
                    maxima(s, n % 2)
                if on(n, LAG_X1):
                    stats(s - LAG_X1, (n - LAG_X1) % 2)
                if on(n, 0):
                    shift(s, n % 2)
                if on(n, LAG_X1):
                    aggregate(s - LAG_X1, (n - LAG_X1) % 2)
                if on(n, -2):
                    normalise(s + 2, n % 2)
                if on(n, LAG_XN2):
                    normalise2(s - LAG_XN2, (n - LAG_XN2) % 2)
                if on(n, LAG_G):
                    logits(s - LAG_G)

            dve.wait_ge(rstd1, 2)
            dve.wait_ge(bc_in, 48)
            dve.wait_ge(zero_out, 32)
            step(-2, -2)
            low_b(B_SPLIT - 2, B_SPLIT)
            step(-1, -1)
            low_b(B_SPLIT, HEADS)
            pipe_a(dve, step)

            count = [0]

            def link(ins):
                count[0] += 1
                ins.then_inc(rt, 1)
                dve.wait_ge(rt, count[0])

            r = R
            rev = con[:, C_REV:C_REV + E9].unsqueeze(1).to_broadcast([P, NT, E9])

            def rows(a):
                return a.unsqueeze(2).to_broadcast([P, NT, E9])

            dve.wait_ge(lg_ok, NT)
            dve.wait_ge(xn2_out[0], 16 * NT // 2)
            dve.wait_ge(xn2_out[1], 16 * NT // 2)
            dve.wait_ge(x1_out[0], 16 * NT // 2)
            dve.wait_ge(x1_out[1], 16 * NT // 2)
            dve.wait_ge(w_lo_ok, 4 * EARLY)
            link(dve.tensor_scalar(lg[:], lg[:], Z_ONE, None, ALU.min))
            link(dve.tensor_reduce(r["m"][:, 0], lg[:], AX.X, ALU.max))
            for k, (src, oh) in enumerate(((lg[:], r["oh1"]), (r["lg2"], r["oh2"]))):
                if k:
                    link(dve.scalar_tensor_tensor(out=r["lg2"], in0=r["oh1"], scalar=MASKED, in1=lg[:], op0=ALU.mult,
                                                  op1=ALU.add))
                    ins = dve.tensor_reduce(r["m"][:, 1], r["lg2"], AX.X, ALU.max)
                    link(ins)
                link(dve.tensor_tensor(r["eq"], src, rows(r["m"][:, k]), ALU.is_ge))
                link(dve.tensor_tensor(r["eq"], r["eq"], rev, ALU.mult))
                link(dve.tensor_reduce(r["c"][:, k], r["eq"], AX.X, ALU.max))
                link(dve.tensor_tensor(oh, rev, rows(r["c"][:, k]), ALU.is_equal))
            dve.memset(r["s16"][:, NT, :], 0.0)
            dve.tensor_tensor(r["s16"][:, 0:NT, :], r["oh1"], r["oh2"], ALU.add).then_inc(s16_ok, 1)
            dve.tensor_copy(r["cws"][:, 0:1], r["m"][:, 0, 0:1]).then_inc(m_ok, 1)
            dve.wait_ge(sig_ok, 1)
            link(dve.tensor_tensor(r["wsum"], r["sgm"][:, 0], r["sgm"][:, 1], ALU.add))
            link(dve.tensor_scalar(r["wsum"], r["wsum"], 1e-20, None, ALU.add))
            link(dve.reciprocal(r["wrec"], r["wsum"]))
            link(dve.tensor_tensor(r["cwv"], r["sgm"], r["wrec"].unsqueeze(1).to_broadcast([P, 2, NT]), ALU.mult))
            u1 = r["ueq"][:, 0:1, 0:2 * NT].rearrange("p a q -> p (a q)")
            link(dve.tensor_copy(u1, r["cwv"].rearrange("p k i -> p (k i)")))
            dve.tensor_copy(r["val"][:, 1], u1)
            link(dve.tensor_tensor(r["val"][:, 2], r["cwv"].rearrange("p k i -> p (k i)"), u1, ALU.subtract))
            for k in range(2):
                ins = dve.tensor_copy(r["val"][:, 0, k * NT:(k + 1) * NT], con[:, C_TOK:C_TOK + NT])
            link(ins)
            dve.wait_ge(rank_mm, 1)
            rank = ps[:, 0, 0:(NT + 1) * E9].rearrange("p (i e) -> p i e", e=E9)
            link(dve.tensor_scalar(r["cnti"][:, 0:E9], rank[:, NT, :], float(P - 1), None, ALU.add))
            link(dve.tensor_scalar(r["cnti"][:, 0:E9], r["cnti"][:, 0:E9], 7, None, ALU.logical_shift_right))
            link(dve.tensor_copy(r["ntl"][:, 0:E9], r["cnti"][:, 0:E9]))
            link(dve.tensor_tensor(r["cmul"], con[:, C_LT:C_LT + E9 * E9].rearrange("p (a b) -> p a b", b=E9),
                                   r["ntl"][:, 0:E9].unsqueeze(1).to_broadcast([P, E9, E9]), ALU.mult))
            link(dve.tensor_reduce(r["cin"][:, 0:E9], r["cmul"], AX.X, ALU.add))
            link(dve.tensor_tensor(r["cex"][:, 0:E9], r["cin"][:, 0:E9], r["ntl"][:, 0:E9], ALU.subtract))
            link(dve.scalar_tensor_tensor(out=r["slot"], in0=r["cex"][:, 0:E9].unsqueeze(1).to_broadcast([P, NT, E9]),
                                          scalar=float(P), in1=rank[:, 0:NT, :], op0=ALU.mult, op1=ALU.add))
            for k, oh in enumerate((r["oh1"], r["oh2"])):
                link(dve.tensor_tensor(r["sel"], r["slot"], oh, ALU.mult))
                link(dve.tensor_reduce(r["sl"][:, k], r["sel"], AX.X, ALU.add))
            link(dve.tensor_copy(r["sli"], r["sl"]))
            dve.tensor_scalar(r["pi"], r["sli"], P - 1, None, ALU.bitwise_and)
            link(dve.tensor_scalar(r["ti"], r["sli"], 7, None, ALU.logical_shift_right))
            dve.tensor_copy(r["pf"], r["pi"].rearrange("p k i -> p (k i)"))
            link(dve.tensor_copy(r["tf"], r["ti"].rearrange("p k i -> p (k i)")))
            link(dve.tensor_tensor(r["ueq"], r["tf"].unsqueeze(2).to_broadcast([P, 2 * NT, NF]),
                                   iota16[:, 0:NF].unsqueeze(1).to_broadcast([P, 2 * NT, NF]), ALU.is_equal))
            dve.sem_inc(ueq_ok, 1)
            for v in range(1, 3):
                ins = dve.tensor_tensor(r["u"][:, :, v, :], r["ueq"], r["val"][:, v].unsqueeze(2).to_broadcast([P, 2 * NT, NF]),
                                        ALU.mult)
            ins.then_inc(u_ok, 1)
            for q in range(2 * NT):
                dve.tensor_scalar(vhot[:, q, :], iota16[:], r["pf"][:, q:q + 1], None, ALU.is_equal).then_inc(v_ok, 1)
            dve.wait_ge(map_mm, 1)
            tab = ps[:, 1, 0:3 * NF].rearrange("p (v t) -> p v t", v=3)
            link(dve.tensor_scalar(r["pad"], tab[:, 0], 0.0, con[:, C_P:C_P + 1], ALU.is_equal, ALU.mult))
            dve.scalar_tensor_tensor(out=idx_all[:], in0=tab[:, 0], scalar=float(T), in1=r["pad"], op0=ALU.add,
                                     op1=ALU.add).then_inc(idx_ok, 1)
            link(dve.tensor_tensor(r["ecmp"], con[:, C_IOTA:C_IOTA + NF].unsqueeze(2).to_broadcast([P, NF, E9]),
                                   r["cin"][:, 0:E9].unsqueeze(1).to_broadcast([P, NF, E9]), ALU.is_ge))
            link(dve.tensor_reduce(r["ef"], r["ecmp"], AX.X, ALU.add))
            link(dve.tensor_scalar(eid[:], r["ef"], float(E9 - 1), None, ALU.min))
            link(dve.tensor_copy(r["cws"], tab[:, 1]))
            link(dve.tensor_tensor(r["cws"], tab[:, 2], r["cws"], ALU.add))
            link(dve.tensor_scalar(cw_all[:], r["cws"], 1.0 / SP_W, None, ALU.mult))
            for k in range(2):
                ins = dve.memset(hb[:, k, HID:HC * P], 0.0)
            ins.then_inc(hpad_ok, 1)
            dve.wait_ge(hpad_ok, 1)
            dve.sem_inc(route_ok, 1)

            def last_low(part):
                dve.wait_ge(w_lo_ok, 4 * (E9 - 1))
                dve.wait_ge(w_hi_ok, 4 * (E9 - 1) + part + 1)
                dve.scalar_tensor_tensor(out=w_chunk(E9 - 1, part, 1), in0=stage[:, part, :], scalar=SP_W,
                                         in1=w_chunk(E9 - 1, part, 0), op0=ALU.mult, op1=ALU.subtract).then_inc(w_lo_ok, 1)

            def fx_low(t, par):
                dve.wait_ge(fxh_ok, t + 1)
                dve.tensor_tensor(fx_l[:, par], ps[:, 6, 0:D].rearrange("p (k t) -> p k t", k=KD), fx_h[:, par],
                                  ALU.subtract).then_inc(fxl_ok, 1)

            def hidden(t, par):
                at_least(dve, fht_mm, 2 * (t - 1))
                for c in range(2):
                    dve.wait_ge(silu_ok, 2 * t + c + 1)
                    dve.wait_ge(w13_mm, 4 * t + c + 3)
                    dve.scalar_tensor_tensor(out=hb[:, par, c * HID // 2:(c + 1) * HID // 2], in0=ps[:, 2 + c, 0:HID // 2],
                                             scalar=1.0 / SP_W, in1=sg[:, par, c * HID // 2:(c + 1) * HID // 2],
                                             op0=ALU.mult, op1=ALU.mult).then_inc(h_ok, 1)

            def fh_low(t):
                for g, (c0, c1) in enumerate(((0, 4), (4, 6))):
                    dve.wait_ge(fhh_ok, 2 * t + g + 1)
                    dve.tensor_tensor(ht_l[:, c0:c1, :], ps[:, 4 + g, 0:(c1 - c0) * P].rearrange("p (c t) -> p c t", t=P),
                                      ht_h[:, c0:c1, :], ALU.subtract).then_inc(fhl_ok, 1)

            def weigh(t, par):
                dve.wait_ge(w2_mm, t + 1)
                at_least(dve, s_out[par], (t // 2) * 16)
                col = slice(t, t + 1) if isinstance(t, int) else bass.ds(t, 1)
                dve.tensor_scalar(yb[:, par], ps[:, 7, 0:D], cw_all[:, col], None, ALU.mult).then_inc(y_ok, 1)

            def fstep(s, n):
                if onf(n, 1):
                    fh_low(s - 1)
                if onf(n, -1):
                    fx_low(s + 1, (n + 1) % 2)
                if onf(n, 2):
                    weigh(s - 2, n % 2)
                if onf(n, 0):
                    hidden(s, n % 2)
                if 0 <= n < 4:
                    last_low(n)

            pipe_f(dve, fstep)

        @block.gpsimd
        def _(pool):
            pool.wait_ge(mask_in, 16)
            pool.tensor_scalar(maskb, mask8, MASKED, None, ALU.mult).then_inc(mask_ok, 1)
            pool.wait_ge(wo_hi_ok, 1)
            pool.tensor_tensor(wo_l, wo_sb, wo_h, ALU.subtract).then_inc(wo_lo_ok, 1)
            pool.wait_ge(stat1_ok, 1)
            pool.wait_ge(cpy, 1)
            pool.tensor_scalar(rstd_all[:], mv_all[:, :, 1], LN_EPS, None, ALU.add).then_inc(rstd1, 1)
            pool.wait_ge(rstd1, 1)
            pool.tensor_tensor(rstd_all[:], rstd_all[:], mhalf[:], ALU.pow).then_inc(rstd1, 1)
            pool.wait_ge(bc_in, 48)

            def w_low(e, part):
                pool.wait_ge(w_hi_ok, e * 4 + (part + 1))
                pool.tensor_tensor(w_chunk(e, part, 1), stage[:, part, :], w_chunk(e, part, 0),
                                   ALU.subtract).then_inc(w_lo_ok, 1)

            def norm(i, par):
                pool.wait_ge(rec_ok, i + 1)
                e3 = ebuf[par][:, 0:HJ].rearrange("p (h j) -> p h j", j=J)
                pool.tensor_tensor(e3, e3, rr[:, par].unsqueeze(2).to_broadcast([P, HEADS, J]), ALU.mult).then_inc(norm_ok, 1)

            def bias(i, par):
                pool.wait_ge(xr_in[par], (i // 2) * 16 + 16)
                pool.tensor_tensor(xrb[:, par], xrb[:, par], bo_b[:], ALU.add).then_inc(xb_ok, 1)

            def rstd(i, par):
                pool.wait_ge(mv_ok, i + 1)
                pool.tensor_tensor(ve2[:, par], mv2[:, par, 1:2], eps[:], ALU.add).then_inc(ve_ok, 1)
                pool.wait_ge(ve_ok, i + 1)
                pool.tensor_tensor(rstd2[:, par], ve2[:, par], mhalf[:, 0:1], ALU.pow).then_inc(rstd_ok, 1)

            def step(s, n):
                if on(n, 2):
                    bias(s - 2, n % 2)
                if on_w(n - 1):
                    w_low((s - 1 - W_STEP) // 2, chunk_parts(n - 1)[0])
                if on(n, 1):
                    norm(s - 1, (n - 1) % 2)
                if on_w(n - 1):
                    w_low((s - 1 - W_STEP) // 2, chunk_parts(n - 1)[1])
                if n == LATE_SPLIT + 2:
                    for part in range(4):
                        w_low(EARLY, part)
                if on(n, LAG_X1):
                    rstd(s - LAG_X1, (n - LAG_X1) % 2)

            prologue_steps(step)
            pipe_a(pool, step)
            for part in range(4):
                if part == U_AT:
                    pool.wait_ge(ueq_ok, 1)
                    pool.tensor_tensor(R["u"][:, :, 0, :], R["ueq"], R["val"][:, 0].unsqueeze(2).to_broadcast([P, 2 * NT, NF]),
                                       ALU.mult).then_inc(u_ok, 1)
                w_low(EARLY + 1, part)
            pool.wait_ge(idx_ok, 1)
            pool.wait_ge(zero_out, 32)

            def gather(t, par):
                at_least(pool, g_in[par], (t // 2) * 16)
                at_least(pool, fxt_mm, t - 1)
                col = slice(t, t + 1) if isinstance(t, int) else bass.ds(t, 1)
                pool.tensor_copy(idg[:, par], idx_all[:, col]).then_inc(idg_ok, 1)
                pool.wait_ge(idg_ok, t + 1)
                pool.sem_inc(dma_go, 1)
                pool.indirect_dma_start(out=xg[:, par], out_offset=None, in_=xn2_rows,
                                        in_offset=bass.IndirectOffsetOnAxis(ap=idg[:, par], axis=0)).then_inc(g_in[par], 16)

            def scatter(t, par):
                at_least(pool, s_out[par], (t // 2) * 16)
                col = slice(t, t + 1) if isinstance(t, int) else bass.ds(t, 1)
                pool.tensor_copy(ids[:, par], idx_all[:, col]).then_inc(ids_ok, 1)
                pool.wait_ge(ids_ok, t + 1)
                pool.wait_ge(y_ok, t + 1)
                at_least(pool, s_out[1 - par], ((t + 1) // 2) * 16)
                pool.sem_inc(dma_go, 1)
                pool.indirect_dma_start(out=acc, out_offset=bass.IndirectOffsetOnAxis(ap=ids[:, par], axis=0), in_=yb[:, par],
                                        in_offset=None, compute_op=ALU.add).then_inc(s_out[par], 16)

            def fstep(s, n):
                if onf(n, 3):
                    scatter(s - 3, (n - 3) % 2)
                if onf(n, -2):
                    gather(s + 2, n % 2)

            pipe_f(pool, fstep)


def shape_constants():
    c = np.zeros((P, C_ALL), np.float32)
    p = np.arange(P)
    c[:, C_ID:C_ID + P] = np.eye(P)
    c[:, C_TRI:C_TRI + P] = p[:, None] < p[None, :]
    c[:, C_IOTA:C_IOTA + P] = p[None, :]
    c[:, C_REV:C_REV + E9] = E9 - np.arange(E9)
    c[:, C_LT:C_LT + E9 * E9] = (np.arange(E9)[None, :] <= np.arange(E9)[:, None]).reshape(-1)
    c[:, C_TOK:C_TOK + NT] = np.arange(NT)[None, :] * P + p[:, None] - T
    c[:, C_P] = p
    return c


def kernel(**inputs):
    import concourse.bacc as bacc
    from concourse.bass_utils import run_bass_kernel_spmd

    a = {k: np.asarray(v) for k, v in inputs.items()}
    w1 = np.concatenate([a["L0_ffn_w1"], a["L0_ffn_new_w1"]])
    w2 = np.concatenate([a["L0_ffn_w2"], a["L0_ffn_new_w2"]])
    w3 = np.concatenate([a["L0_ffn_w3"], a["L0_ffn_new_w3"]])
    w13 = np.concatenate([w1, w3], axis=1).reshape(E9, 2 * HID, KD, P).transpose(0, 3, 2, 1).reshape(E9, P, W13C)
    w2t = np.concatenate([w2.transpose(0, 2, 1), np.zeros((E9, HC * P - HID, D), np.float32)], axis=1)
    w2t = w2t.reshape(E9, HC, P, D).transpose(0, 2, 1, 3).reshape(E9, P, HC * D)
    arrays = {
        "x": a["x"].reshape(T, D),
        "ctxT": a["ctx_1024"].reshape(B * J, D).T,
        "mask": np.ascontiguousarray(a["mask_BxSxS2_bk1"].reshape(NT, P, J).transpose(1, 0, 2)).reshape(P, NT * J).view(np.uint32),
        "wq": a["L0_xattn_Wq"].T,
        "wk": a["L0_xattn_Wk"],
        "wv": a["L0_xattn_Wv"],
        "wo": a["L0_xattn_Wo"],
        "bo": a["L0_xattn_bo"],
        "wt": np.concatenate([w13, w2t], axis=2),
        "gate": np.concatenate([a["L0_ffn_gate_weight"], a["L0_ffn_new_gate_weight"]]).T,
        "gbias": np.concatenate([np.zeros(E9 - 1, np.float32), a["L0_ffn_gate_bias"]]),
        "consts": shape_constants(),
    }
    nc = bacc.Bacc("TRN2", target_bir_lowering=False, num_devices=1)
    ins, args = {}, []
    for name, v in arrays.items():
        v = np.ascontiguousarray(v)
        ins["in_" + name] = v
        args.append(nc.dram_tensor("in_" + name, v.shape, mybir.dt.from_np(v.dtype), kind="ExternalInput").ap())
    out = nc.dram_tensor("out_rows", (TR, D), F32, kind="ExternalOutput").ap()
    build(nc, *args, out)
    r = run_bass_kernel_spmd(nc, [ins], core_ids=[0])
    return r.results[0]["out_rows"][:T].reshape(B, N, D)
```
